# Optimizing a Trainium2 kernel written in Bass

```python
import numpy as np
import jax
import jax.numpy as jnp

def _softmax(x, axis=-1):
    return jax.nn.softmax(x, axis=axis)

def _gelu(x):
    return jax.nn.gelu(x, approximate=True)

def _silu(x):
    return jax.nn.silu(x)

def _sigmoid(x):
    return jax.nn.sigmoid(x)

def _layernorm(x, axis=-1, eps=1e-05):
    m = jnp.mean(x, axis=axis, keepdims=True)
    v = jnp.var(x, axis=axis, keepdims=True)
    return (x - m) / jnp.sqrt(v + eps)

def _scatter_add(tgt, idx, src, axis=0):
    return tgt.at[idx].add(src)

def _segment_sum(src, seg, n):
    return jax.ops.segment_sum(src, seg, n)
kernel_name = 'mk_sandwich_d1_jaxref_r4_2bf901'

def setup_inputs(seed: int=0):
    np.random.seed(seed)
    _w = jnp.asarray

    def _L0_attn_setup():
        import jax, jax.numpy as jnp
        import numpy as np
        B, T, D, H = (2, 512, 256, 4)
        DK, DV = (256, 512)
        HK, HV = (DK // H, DV // H)
        LR = 16
        EPS = 1e-05
        GATE_NORM = 16.0

        def _xavier(k, shape, gain):
            fan_in, fan_out = shape
            lim = gain * np.sqrt(6.0 / (fan_in + fan_out))
            return jax.random.uniform(k, shape, jnp.float32, -lim, lim)

        def _gla_scan(q, k, v, g):
            S0 = jnp.zeros((q.shape[-1], v.shape[-1]), q.dtype)

            def step(S, inp):
                qt, kt, vt, gt = inp
                S = jnp.exp(gt)[:, None] * S + kt[:, None] * vt[None, :]
                return (S, qt @ S)
            return jax.lax.scan(step, S0, (q, k, v, g))[1]

        def _forward(x, Wq, Wk, Wv, Wg, gk_w1, gk_w2, gk_b, Wo, rms_w):
            b, t = (x.shape[0], x.shape[1])
            scale = HK ** (-0.5)
            q = (x @ Wq).reshape(b, t, H, HK).transpose(0, 2, 1, 3) * scale
            k = (x @ Wk).reshape(b, t, H, HK).transpose(0, 2, 1, 3)
            v = (x @ Wv).reshape(b, t, H, HV).transpose(0, 2, 1, 3)
            gl = x @ gk_w1 @ gk_w2 + gk_b
            g = jax.nn.log_sigmoid(gl.astype(jnp.float32)) / GATE_NORM
            g = g.reshape(b, t, H, HK).transpose(0, 2, 1, 3)
            o = jax.vmap(jax.vmap(_gla_scan))(q, k, v, g)
            o = o.transpose(0, 2, 1, 3)
            o = o * jax.lax.rsqrt(jnp.mean(o * o, axis=-1, keepdims=True) + EPS) * rms_w
            o = o.reshape(b, t, DV) * jax.nn.silu(x @ Wg)
            return o @ Wo
        key = jax.random.key(seed)
        ks = jax.random.split(key, 10)
        g_qkv = 2 ** (-2.5)
        return {'x': jax.random.normal(ks[0], (B, T, D), jnp.float32), 'Wq': _xavier(ks[1], (D, DK), g_qkv), 'Wk': _xavier(ks[2], (D, DK), g_qkv), 'Wv': _xavier(ks[3], (D, DV), g_qkv), 'Wg': _xavier(ks[4], (D, DV), g_qkv), 'gk_w1': _xavier(ks[5], (D, LR), g_qkv), 'gk_w2': _xavier(ks[6], (LR, DK), g_qkv), 'gk_b': jnp.zeros((DK,), jnp.float32), 'Wo': _xavier(ks[7], (DV, D), 2 ** (-1)), 'rms_w': jnp.ones((HV,), jnp.float32)}
    _L0_attn_in = _L0_attn_setup()

    def _L0_ffn_setup():
        import jax, jax.numpy as jnp
        import numpy as np
        NUM_EXPERTS = 8
        D_MODEL = 256
        D_FF = 1024
        BATCH, SEQ = (2, 1024)
        key = jax.random.key(seed)
        k_x, k_w1, k_w2 = jax.random.split(key, 3)
        x = jax.random.normal(k_x, (BATCH, SEQ, D_MODEL), dtype=jnp.float32)
        w1 = jax.random.normal(k_w1, (NUM_EXPERTS, D_MODEL, D_FF), dtype=jnp.float32) * (1.0 / np.sqrt(D_MODEL))
        b1 = jnp.zeros((NUM_EXPERTS, D_FF), dtype=jnp.float32)
        w2 = jax.random.normal(k_w2, (NUM_EXPERTS, D_FF, D_MODEL), dtype=jnp.float32) * (1.0 / np.sqrt(D_FF))
        b2 = jnp.zeros((NUM_EXPERTS, D_MODEL), dtype=jnp.float32)
        return {'x': x, 'w1': w1, 'b1': b1, 'w2': w2, 'b2': b2}
    _L0_ffn_in = _L0_ffn_setup()
    _d = {'L0_attn_x': _L0_attn_in['x'], 'L0_attn_Wq': _L0_attn_in['Wq'], 'L0_attn_Wk': _L0_attn_in['Wk'], 'L0_attn_Wv': _L0_attn_in['Wv'], 'L0_attn_Wg': _L0_attn_in['Wg'], 'L0_attn_gk_w1': _L0_attn_in['gk_w1'], 'L0_attn_gk_w2': _L0_attn_in['gk_w2'], 'L0_attn_gk_b': _L0_attn_in['gk_b'], 'L0_attn_Wo': _L0_attn_in['Wo'], 'L0_attn_rms_w': _L0_attn_in['rms_w'], 'L0_ffn_w1': _L0_ffn_in['w1'], 'L0_ffn_b1': _L0_ffn_in['b1'], 'L0_ffn_w2': _L0_ffn_in['w2'], 'L0_ffn_b2': _L0_ffn_in['b2']}
    _x0 = _d['L0_attn_x']
    _d['L0_attn_x'] = jax.random.normal(jax.random.fold_in(jax.random.key(seed), 1), (16, 512, 256), dtype=_x0.dtype)
    del _x0
    return _d

def reference(L0_attn_x, L0_attn_Wq, L0_attn_Wk, L0_attn_Wv, L0_attn_Wg, L0_attn_gk_w1, L0_attn_gk_w2, L0_attn_gk_b, L0_attn_Wo, L0_attn_rms_w, L0_ffn_w1, L0_ffn_b1, L0_ffn_w2, L0_ffn_b2):

    def _L0_attn_ref(x, Wq, Wk, Wv, Wg, gk_w1, gk_w2, gk_b, Wo, rms_w):
        import jax, jax.numpy as jnp
        import numpy as np
        B, T, D, H = (2, 512, 256, 4)
        DK, DV = (256, 512)
        HK, HV = (DK // H, DV // H)
        LR = 16
        EPS = 1e-05
        GATE_NORM = 16.0

        def _xavier(k, shape, gain):
            fan_in, fan_out = shape
            lim = gain * np.sqrt(6.0 / (fan_in + fan_out))
            return jax.random.uniform(k, shape, jnp.float32, -lim, lim)

        def _gla_scan(q, k, v, g):
            S0 = jnp.zeros((q.shape[-1], v.shape[-1]), q.dtype)

            def step(S, inp):
                qt, kt, vt, gt = inp
                S = jnp.exp(gt)[:, None] * S + kt[:, None] * vt[None, :]
                return (S, qt @ S)
            return jax.lax.scan(step, S0, (q, k, v, g))[1]

        def _forward(x, Wq, Wk, Wv, Wg, gk_w1, gk_w2, gk_b, Wo, rms_w):
            b, t = (x.shape[0], x.shape[1])
            scale = HK ** (-0.5)
            q = (x @ Wq).reshape(b, t, H, HK).transpose(0, 2, 1, 3) * scale
            k = (x @ Wk).reshape(b, t, H, HK).transpose(0, 2, 1, 3)
            v = (x @ Wv).reshape(b, t, H, HV).transpose(0, 2, 1, 3)
            gl = x @ gk_w1 @ gk_w2 + gk_b
            g = jax.nn.log_sigmoid(gl.astype(jnp.float32)) / GATE_NORM
            g = g.reshape(b, t, H, HK).transpose(0, 2, 1, 3)
            o = jax.vmap(jax.vmap(_gla_scan))(q, k, v, g)
            o = o.transpose(0, 2, 1, 3)
            o = o * jax.lax.rsqrt(jnp.mean(o * o, axis=-1, keepdims=True) + EPS) * rms_w
            o = o.reshape(b, t, DV) * jax.nn.silu(x @ Wg)
            return o @ Wo
        return _forward(x, Wq, Wk, Wv, Wg, gk_w1, gk_w2, gk_b, Wo, rms_w)

    def _L0_ffn_ref(x, w1, b1, w2, b2):
        import jax, jax.numpy as jnp
        import numpy as np
        NUM_EXPERTS = 8
        D_MODEL = 256
        D_FF = 1024
        BATCH, SEQ = (2, 1024)
        B, S, D = x.shape
        E = w1.shape[0]
        T = B * S // E
        tokens = x.reshape(E, T, D)
        h = jnp.einsum('etd,edf->etf', tokens, w1) + b1[:, None, :]
        h = jax.nn.gelu(h)
        y = jnp.einsum('etf,efd->etd', h, w2) + b2[:, None, :]
        return y.reshape(B, S, D)
    x = L0_attn_x
    x = x + _layernorm(_L0_attn_ref(_layernorm(x, axis=-1), L0_attn_Wq, L0_attn_Wk, L0_attn_Wv, L0_attn_Wg, L0_attn_gk_w1, L0_attn_gk_w2, L0_attn_gk_b, L0_attn_Wo, L0_attn_rms_w), axis=-1)
    x = x + _layernorm(_L0_ffn_ref(_layernorm(x, axis=-1), L0_ffn_w1, L0_ffn_b1, L0_ffn_w2, L0_ffn_b2), axis=-1)
    return x

_drawn_inputs = setup_inputs


def setup_inputs(seed=0):
    import zlib

    import numpy as np

    out = dict(_drawn_inputs(seed))
    spreads = {'L0_attn_gk_b': (0.0, 0.1),
     'L0_attn_rms_w': (1.0, 0.2),
     'L0_ffn_b1': (0.0, 0.1),
     'L0_ffn_b2': (0.0, 0.1)}
    factors = {'L0_attn_gk_w1': 8.0, 'L0_attn_gk_w2': 8.0}
    for name, (base, spread) in spreads.items():
        noise = np.random.default_rng([zlib.crc32(name.encode()), seed]).standard_normal(out[name].shape)
        drawn = base * np.exp(spread * noise) if base else spread * noise
        out[name] = jnp.asarray(drawn.astype(out[name].dtype))
    for name, factor in factors.items():
        out[name] = (out[name] * factor).astype(out[name].dtype)
    return out
```

```python
def build(nc, x_d, wq_d, wk_d, wv_d, wg_d, w1t_d, w2g_d, gkb_d, wo_d, rms_d,
          fw1_d, fb1_d, fw2_d, fb2_d, out_d):
    from contextlib import ExitStack
    from concourse import mybir

    F32, F32R, U32 = mybir.dt.float32, mybir.dt.float32r, mybir.dt.uint32
    ACT, ALU = mybir.ActivationFunctionType, mybir.AluOpType
    P = 128
    NB, T, D = x_d.shape
    E, _, DF = fw1_d.shape
    LR = w2g_d.shape[0]
    DV = wv_d.shape[1]
    H = 4
    HV = DV // H
    HK = D // H
    CH = 128
    NCH = T // CH
    KT = D // P
    FT = DF // P
    VT = DV // P
    LV = [1, 2, 4, 8, 16, 32, 64]
    NL = len(LV)
    MASKED = 5
    HC = CH // 2
    EPS = 1e-5
    QSCALE = HK ** -0.5
    GATE_NORM = 16.0
    SLOTS = NB

    ctx = ExitStack()
    with ctx:
        def sb(name, shape, dt=F32):
            return ctx.enter_context(nc.sbuf_tensor(name, shape, dt))

        def ps(name):
            return ctx.enter_context(nc.psum_tensor(name, [P, 512], F32))

        xb = [sb(f"x_in{j}", [P, NCH, D]) for j in range(2)]
        xh = sb("x_normed", [P, NCH, D])
        xT_hi, xT_lo = sb("xT_hi", [P, KT, T], F32R), sb("xT_lo", [P, KT, T], F32R)
        x2 = sb("x_mid", [P, NCH, D])
        y = sb("y", [P, NCH, D])
        qbd = sb("q_blockdiag", [P, KT, 2, T])
        kk = sb("k_decayed", [P, KT, T])
        ga = sb("gates", [P, KT, T])
        qk = sb("q_times_k", [P, KT, T])
        gn = qk
        tot = sb("block_totals", [P, KT, T])
        Am = sb("attn_T", [P, KT, NCH * 2, CH])
        kT = sb("k_tokens", [P, NCH, D])
        S = sb("state", [P, KT, HV])
        v = sb("v", [P, NCH, DV])
        gs = sb("out_gate", [P, NCH, DV])
        o = sb("o", [P, DV])
        ogT_hi, ogT_lo = sb("ogT_hi", [P, VT, CH], F32R), sb("ogT_lo", [P, VT, CH], F32R)
        hf = sb("gelu_out", [P, 2, T])
        gm = hf
        h_hi, h_lo = sb("h_hi", [P, FT, T], F32R), sb("h_lo", [P, FT, T], F32R)
        NA = 3 * D
        WA = [sb(f"w_qkg_{n}", [P, KT, NA], F32R) for n in ("hi", "lo")]
        WB = [sb(f"w_vg_{n}", [P, KT, 2 * DV], F32R) for n in ("hi", "lo")]
        WO = [sb(f"w_o_{n}", [P, VT, D], F32R) for n in ("hi", "lo")]
        W1 = [sb(f"w_ff1_{n}", [P, KT, DF], F32R) for n in ("hi", "lo")]
        W2 = [sb(f"w_ff2_{n}", [P, FT, D], F32R) for n in ("hi", "lo")]
        RAW = KT * DF
        raw = sb("w_raw", [P, RAW])
        masks = sb("level_masks", [P, MASKED, HC])
        rmsb = sb("rms_w_rows", [P, DV])
        b2s = sb("ff_b2_rows", [P, D])
        b1s = sb("ff_b1_cols", [P, FT])
        gkb = sb("gk_b_cols", [P, KT])
        ident = sb("ident", [P, P])
        ind = sb("head_sum", [P, 2])
        mhalf = sb("minus_half", [P, NCH * H])
        stat = sb("bn", [P, 4, NCH, 6])
        mv = sb("mean_var", [P, 4, NCH, 2])
        rs = sb("rstd", [P, 4, NCH])
        nm = sb("minus_mean_rstd", [P, 4, NCH])
        ssq = sb("o_sumsq", [P, NCH * H])
        rso = sb("o_rstd", [P, NCH * H])
        dg = sb("qk_diag", [P, NCH * H])
        junk = sb("square_out", [P, DV])
        w1t = raw[0:LR, 0:D]
        w2g = raw[0:LR, D:2 * D]

        PB = [ps(f"ps_big{j}") for j in range(2)]
        PT = [ps(f"ps_transpose{j}") for j in range(2)]
        PL = [ps(f"ps_level{j}") for j in range(2)]
        PO, PS = ps("ps_out"), ps("ps_state")

        toff, at = {}, 0
        for h in LV[1:] + [CH]:
            toff[h] = at
            at += T // h

        def totals(h):
            return ga[:, :, :] if h == 1 else tot[:, :, toff[h]:toff[h] + T // h]

        PER = dict(
            x_in=16, st_out=16, w_in=32, b_in=32,
            pe_diag=1, pe_lv=2 * NL, pe_x3t=KT, pe_f1=FT, pe_f2=NCH, pe_kt=2, pe_xt=KT, pe_gl=KT,
            pe_k=KT, pe_q=KT, pe_v=NCH, pe_g=NCH, pe_st=NCH - 1, pe_att=NCH, pe_ogt=NCH, pe_wo=NCH,
            dv_dg=1, dv_ln1=2 * NCH, dv_ln2=2 * NCH, dv_ln3=2 * NCH, dv_ln4=2 * NCH, dv_x3lo=KT,
            dv_cp=2 * MASKED, dv_qu=4 * NL, dv_hlo=FT, dv_y4=NCH, dv_xlo=KT, dv_gl=KT, dv_gsub=1,
            dv_tot=NL, dv_q=3 * KT, dv_st=4 * (NCH - 1), dv_o=NCH * H, dv_og=NCH * H, dv_oglo=NCH,
            ac_t=NCH, ac_xh3=NCH, ac_x3hi=KT, ac_gelu=FT, ac_fin=NCH, ac_cp=6, ac_kt=2, ac_xhi=KT,
            ac_abs=KT, ac_e=1, ac_l=1, ac_a=1, ac_k=KT, ac_v=NCH, ac_g=NCH, ac_sq=NCH * H, ac_oghi=NCH, ac_y=NCH,
            po_ln1=4, po_ln2=4, po_ln3=4, po_ln4=4, po_x2=1, po_ku=2 * NL, po_hhi=FT, po_fin=1,
            po_xh=NCH, po_gw=NCH, po_ro=2 * NCH, po_ws=4,
        )
        sem = {n: ctx.enter_context(nc.semaphore(n)) for n in PER}
        c_in = ctx.enter_context(nc.semaphore("const_in"))
        c_ready = ctx.enter_context(nc.semaphore("const_ready"))
        c_step = ctx.enter_context(nc.semaphore("const_step"))
        c_split = ctx.enter_context(nc.semaphore("const_split"))
        c_w12 = ctx.enter_context(nc.semaphore("const_w12"))

        def at(name, b, c):
            return b * PER[name] + c

        def own_wait(eng, b):
            if not isinstance(b, int):
                eng.nop(nofuse=True)

        def program(eng, run):
            run(-1, 1, 0, False, False, True)
            run(0, 0, 0, True, False, True)
            with eng.Fori(0, NB // 2 - 1) as i:
                run(i * 2 + 1, 1, i, True, True, True)
                run(i * 2 + 2, 0, i, True, True, True)
            run(NB - 1, 1, E - 1, True, True, False)
            run(NB, 0, E - 1, False, True, False)

        def halves(ap, h):
            return ap.rearrange("p (n t h) -> p n t h", t=2, h=h)

        block = ctx.enter_context(nc.Block())

        @block.sync
        def _(sp):
            sp.dma_start(gkb[:, :], gkb_d).then_inc(c_in, 16)
            sp.dma_start(rmsb[:, :], rms_d).then_inc(c_in, 16)
            sp.dma_start(w1t, w1t_d).then_inc(c_in, 16)
            sp.dma_start(w2g, w2g_d).then_inc(c_in, 16)
            sp.dma_start(xb[0][:, :, :], x_d[0].rearrange("(c p) d -> p c d", p=P)).then_inc(sem["x_in"], 16)
            parts = [(raw[:, 0:KT * 2 * D].rearrange("p (k n) -> p k n", k=KT), [wq_d, wk_d]),
                     (raw[:, 0:KT * 2 * DV].rearrange("p (k n) -> p k n", k=KT)[:, :, 0:2 * DV], [wv_d, wg_d]),
                     (raw[:, 0:VT * D].rearrange("p (k n) -> p k n", k=VT), [wo_d])]
            for n, (dst, srcs) in enumerate(parts):
                sp.wait_ge(c_split, 2 * n + 2)
                w = srcs[0].shape[1]
                for m, src in enumerate(srcs):
                    sp.dma_start(dst[:, :, m * w:(m + 1) * w],
                                 src.rearrange("(k p) n -> p k n", p=P)).then_inc(c_in, 16)

            def load_w1(e, s, C):
                sp.dma_start(raw[:, :].rearrange("p (k n) -> p k n", k=KT),
                             fw1_d[e].rearrange("(k p) n -> p k n", p=P)).then_inc(sem["w_in"], 16)
                if C:
                    sp.wait_ge(sem["ac_gelu"], at("ac_gelu", s - 1, FT))
                    sp.wait_ge(sem["dv_y4"], at("dv_y4", s - 1, NCH))
                sp.dma_start(b1s[:, :], fb1_d[e]).then_inc(sem["b_in"], 16)
                sp.dma_start(b2s[:, :], fb2_d[e]).then_inc(sem["b_in"], 16)

            def load_w2(e):
                sp.wait_ge(sem["po_ws"], at("po_ws", e, 2))
                sp.dma_start(raw[:, :].rearrange("p (k n) -> p k n", k=FT),
                             fw2_d[e].rearrange("(k p) n -> p k n", p=P)).then_inc(sem["w_in"], 16)

            def run(s, j, e, B, C, A):
                if B and A:
                    if C:
                        sp.wait_ge(sem["po_x2"], at("po_x2", s - 1, 1))
                    sp.dma_start(xb[1 - j][:, :, :],
                                 x_d[s + 1].rearrange("(c p) d -> p c d", p=P)).then_inc(sem["x_in"], 16)
                if B and A and j == 0:
                    if isinstance(s, int):
                        sp.wait_ge(c_split, 8)
                        load_w1(0, s, C)
                    else:
                        sp.wait_ge(sem["po_ws"], at("po_ws", e, 4))
                        load_w1(e + 1, s, C)
                if C:
                    sp.wait_ge(sem["po_fin"], at("po_fin", s - 1, 1))
                    sp.dma_start(out_d[s - 1].rearrange("(c p) d -> p c d", p=P),
                                 y[:, :, :]).then_inc(sem["st_out"], 16)
                if B and A and j == 0:
                    load_w2(0 if isinstance(s, int) else e + 1)

            program(sp, run)
            sp.wait_ge(sem["st_out"], 16 * NB)

        @block.tensor
        def _(pe):
            def three(out, lhs, rhs):
                n = len(lhs)
                for i in range(n):
                    (ah, al), (bh, bl) = lhs[i], rhs[i]
                    nc.tensor.matmul(out, ah, bh, start=(i == 0), stop=False)
                    nc.tensor.matmul(out, ah, bl, start=False, stop=False)
                    last = nc.tensor.matmul(out, al, bh, start=False, stop=(i == n - 1))
                return last

            pe.wait_ge(c_ready, 3)
            pe.wait_ge(c_in, 64)
            for kt in range(KT):
                last = nc.tensor.matmul(PB[0][:, kt * D:(kt + 1) * D], w1t[:, kt * P:(kt + 1) * P],
                                        w2g, start=True, stop=True)
            last.then_inc(c_w12, 1)
            pe.wait_ge(c_split, 8)

            def transpose_tokens(src, kt):
                for c in range(NCH):
                    last = nc.tensor.transpose(PT[kt][:, c * P:(c + 1) * P],
                                               src[:, c, kt * P:(kt + 1) * P], ident[:, :])
                return last

            def run(s, j, e, B, C, A):
                p, n = s - 1, s + 1

                def level(i, tl):
                    h = LV[i]
                    if i == 0:
                        if tl == 0:
                            pe.wait_ge(sem["dv_q"], at("dv_q", s, 3 * KT))
                            pe.wait_ge(sem["ac_k"], at("ac_k", s, KT))
                        if C:
                            pe.wait_ge(sem["ac_y"], at("ac_y", p, 3 + tl))
                    else:
                        pe.wait_ge(sem["dv_qu"], at("dv_qu", s, 4 * (i - 1) + 2 * tl + 2))
                        pe.wait_ge(sem["po_ku"], at("po_ku", s, 2 * (i - 1) + tl + 1))
                        if i - 1 < MASKED:
                            pe.wait_ge(sem["dv_cp"], at("dv_cp", s, 2 * (i - 1) + tl + 1))
                        else:
                            pe.wait_ge(sem["ac_cp"], at("ac_cp", s, 2 * tl + 2))
                    for c in range(NCH):
                        q = qbd[:, tl, :, c * CH:(c + 1) * CH].rearrange("p a (n t h) -> p a n t h", t=2, h=h)
                        last = nc.tensor.matmul(PL[tl][:, c * CH:(c + 1) * CH],
                                                kk[:, tl, c * CH:(c + 1) * CH], q[:, :, :, 1, :],
                                                start=True, stop=True)
                    last.then_inc(sem["pe_lv"], 1)

                def diag():
                    pe.wait_ge(sem["dv_q"], at("dv_q", s, 3 * KT))
                    if C:
                        pe.wait_ge(sem["dv_o"], at("dv_o", p, NCH * H))
                    for c in range(NCH):
                        for tl in range(KT):
                            w = c * H + 2 * tl
                            last = nc.tensor.matmul(PO[:, w:w + 2], qk[:, tl, c * CH:(c + 1) * CH],
                                                    ind[:, :], start=True, stop=True)
                    last.then_inc(sem["pe_diag"], 1)

                def x3t(kt):
                    pe.wait_ge(sem["ac_xh3"], at("ac_xh3", p, NCH))
                    pe.wait_ge(sem["dv_oglo"], at("dv_oglo", p, 3 + kt))
                    transpose_tokens(xh, kt).then_inc(sem["pe_x3t"], 1)

                def f1(m):
                    pe.wait_ge(sem["dv_x3lo"], at("dv_x3lo", p, KT))
                    pe.wait_ge(sem["po_ws"], at("po_ws", e, 2))
                    if m >= 2:
                        pe.wait_ge(sem["ac_gelu"], at("ac_gelu", p, m - 1))
                    elif B and m == 0:
                        pe.wait_ge(sem["ac_v"], at("ac_v", s, NCH))
                    elif B:
                        pe.wait_ge(sem["ac_g"], at("ac_g", s, NCH))
                    w = slice(m * P, (m + 1) * P)
                    three(PB[m % 2][:, :], [(W1[0][:, kt, w], W1[1][:, kt, w]) for kt in range(KT)],
                          [(xT_hi[:, kt, :], xT_lo[:, kt, :]) for kt in range(KT)]).then_inc(sem["pe_f1"], 1)

                def f2(c):
                    pe.wait_ge(sem["dv_hlo"], at("dv_hlo", p, FT))
                    pe.wait_ge(sem["po_ws"], at("po_ws", e, 4))
                    if c >= 2:
                        pe.wait_ge(sem["dv_y4"], at("dv_y4", p, c - 1))
                    else:
                        pe.wait_ge(sem["ac_gelu"], at("ac_gelu", p, FT - 1 + c))
                    t = slice(c * CH, (c + 1) * CH)
                    three(PB[c % 2][:, 0:D], [(h_hi[:, m, t], h_lo[:, m, t]) for m in range(FT)],
                          [(W2[0][:, m, :], W2[1][:, m, :]) for m in range(FT)]).then_inc(sem["pe_f2"], 1)

                def kh(f):
                    pe.wait_ge(sem["po_ku"], at("po_ku", s, 2 * NL))
                    if C:
                        pe.wait_ge(sem["dv_x3lo"], at("dv_x3lo", p, f + 1))
                    else:
                        pe.wait_ge(sem["dv_xlo"], at("dv_xlo", s, f + 1))
                    for c in range(2):
                        for tl in range(KT):
                            w = (2 * f + c) * CH
                            last = nc.tensor.transpose(PT[f][:, c * D + tl * P:c * D + (tl + 1) * P],
                                                       kk[:, tl, w:w + CH], ident[:, :])
                    last.then_inc(sem["pe_kt"], 1)

                def xt(kt):
                    pe.wait_ge(sem["po_xh"], at("po_xh", n, NCH))
                    if B:
                        pe.wait_ge(sem["ac_kt"], at("ac_kt", s, kt + 1))
                    transpose_tokens(xh, kt).then_inc(sem["pe_xt"], 1)

                def feature_tile(bank, col):
                    w = slice(col, col + P)
                    return three(bank[:, :], [(WA[0][:, kt, w], WA[1][:, kt, w]) for kt in range(KT)],
                                 [(xT_hi[:, kt, :], xT_lo[:, kt, :]) for kt in range(KT)])

                def token_tile(bank, c, half):
                    t, w = slice(c * CH, (c + 1) * CH), slice(half * DV, (half + 1) * DV)
                    return three(bank[:, :], [(xT_hi[:, kt, t], xT_lo[:, kt, t]) for kt in range(KT)],
                                 [(WB[0][:, kt, w], WB[1][:, kt, w]) for kt in range(KT)])

                def gl(tl):
                    pe.wait_ge(sem["dv_xlo"], at("dv_xlo", n, KT))
                    if C:
                        pe.wait_ge(sem["dv_y4"], at("dv_y4", p, 3 + tl))
                    elif B:
                        pe.wait_ge(sem[("ac_v", "ac_g")[tl]], at(("ac_v", "ac_g")[tl], s, NCH))
                    feature_tile(PB[tl], 2 * D + tl * P).then_inc(sem["pe_gl"], 1)

                def kp(tl):
                    pe.wait_ge(sem["dv_gl"], at("dv_gl", n, tl + 1))
                    feature_tile(PB[tl], D + tl * P).then_inc(sem["pe_k"], 1)

                def qp(tl):
                    pe.wait_ge(sem[("ac_v", "ac_g")[tl]], at(("ac_v", "ac_g")[tl], n, 3))
                    feature_tile(PB[tl], tl * P).then_inc(sem["pe_q"], 1)

                def vp(c):
                    if c == 0:
                        pe.wait_ge(sem["ac_k"], at("ac_k", n, 1))
                    elif c == 3:
                        pe.wait_ge(sem["dv_q"], at("dv_q", n, 3))
                    else:
                        pe.wait_ge(sem["ac_v"], at("ac_v", n, c))
                    token_tile(PB[0], c, 0).then_inc(sem["pe_v"], 1)

                def gp(c):
                    if c == 0:
                        pe.wait_ge(sem["ac_k"], at("ac_k", n, 2))
                    elif c == 3:
                        pe.wait_ge(sem["dv_q"], at("dv_q", n, 6))
                    else:
                        pe.wait_ge(sem["ac_g"], at("ac_g", n, c))
                    token_tile(PB[1], c, 1).then_inc(sem["pe_g"], 1)

                def st(c):
                    pe.wait_ge(sem["ac_kt"], at("ac_kt", s, c // 2 + 1))
                    pe.wait_ge(sem["ac_v"], at("ac_v", s, c + 1))
                    if c:
                        pe.wait_ge(sem["dv_st"], at("dv_st", s, 4 * c))
                    elif C:
                        pe.wait_ge(sem["dv_st"], at("dv_st", p, 4 * (NCH - 1)))
                    for tl in range(KT):
                        last = nc.tensor.matmul(PS[:, tl * 2 * HV:(tl + 1) * 2 * HV],
                                                kT[:, c, tl * P:(tl + 1) * P],
                                                v[:, c, tl * 2 * HV:(tl + 1) * 2 * HV], start=True, stop=True)
                    last.then_inc(sem["pe_st"], 1)

                def att(c):
                    pe.wait_ge(sem["dv_cp"], at("dv_cp", s, 2 * MASKED))
                    pe.wait_ge(sem["ac_cp"], at("ac_cp", s, 6))
                    pe.wait_ge(sem["dv_qu"], at("dv_qu", s, 4 * NL))
                    pe.wait_ge(sem["ac_v"], at("ac_v", s, c + 1))
                    if c:
                        pe.wait_ge(sem["dv_o"], at("dv_o", s, c * H))
                        pe.wait_ge(sem["dv_st"], at("dv_st", s, 4 * c))
                    else:
                        pe.wait_ge(sem["dv_dg"], at("dv_dg", s, 1))
                    for hd in range(H):
                        tl, hh = hd // 2, hd % 2
                        w = slice(hd * HV, (hd + 1) * HV)
                        last = nc.tensor.matmul(PO[:, w], Am[:, tl, 2 * c + hh, :], v[:, c, w],
                                                start=True, stop=(c == 0))
                        if c:
                            last = nc.tensor.matmul(PO[:, w], qbd[:, tl, hh, c * CH:(c + 1) * CH],
                                                    S[:, tl, :], start=False, stop=True)
                    last.then_inc(sem["pe_att"], 1)

                def ogt(c):
                    pe.wait_ge(sem["dv_og"], at("dv_og", s, H * (c + 1)))
                    if c >= 2:
                        pe.wait_ge(sem["dv_oglo"], at("dv_oglo", s, c - 1))
                    elif A:
                        pe.wait_ge(sem["dv_xlo"], at("dv_xlo", n, c + 1))
                    else:
                        pe.wait_ge(sem["ac_kt"], at("ac_kt", s, c + 1))
                    for k in range(VT):
                        last = nc.tensor.transpose(PT[c % 2][:, k * P:(k + 1) * P], o[:, k * P:(k + 1) * P], ident[:, :])
                    last.then_inc(sem["pe_ogt"], 1)

                def wo(c):
                    pe.wait_ge(sem["dv_oglo"], at("dv_oglo", s, c + 1))
                    if c >= 2:
                        pe.wait_ge(sem["ac_y"], at("ac_y", s, c - 1))
                    else:
                        pe.wait_ge(sem["ac_cp"], at("ac_cp", s, 5 + c))
                    three(PL[c % 2][:, 0:D], [(ogT_hi[:, k, :], ogT_lo[:, k, :]) for k in range(VT)],
                          [(WO[0][:, k, :], WO[1][:, k, :]) for k in range(VT)]).then_inc(sem["pe_wo"], 1)

                if B:
                    diag()
                for step in range(2 * NL):
                    if B:
                        level(step // 2, step % 2)
                    if C:
                        if step == 3:
                            x3t(0)
                            x3t(1)
                        if 4 <= step < 4 + FT:
                            f1(step - 4)
                        if step >= 4 + FT:
                            f2(step - 4 - FT)
                if C:
                    f2(2)
                    f2(3)
                if B:
                    kh(0)
                    kh(1)
                if A:
                    xt(0)
                    xt(1)
                    gl(0)
                    gl(1)
                if B:
                    st(0)
                    att(0)
                if A:
                    kp(0)
                    kp(1)
                if B:
                    st(1)
                    att(1)
                if A:
                    vp(0)
                    gp(0)
                if B:
                    ogt(0)
                    st(2)
                    att(2)
                if A:
                    vp(1)
                if B:
                    wo(0)
                if A:
                    gp(1)
                if B:
                    ogt(1)
                    att(3)
                if A:
                    vp(2)
                if B:
                    wo(1)
                if A:
                    gp(2)
                if B:
                    ogt(2)
                if A:
                    qp(0)
                if B:
                    wo(2)
                if A:
                    qp(1)
                if B:
                    ogt(3)
                if A:
                    vp(3)
                    gp(3)
                if B:
                    wo(3)

            program(pe, run)

        @block.vector
        def _(dve):
            def layer_stats(k, src, c, name, b):
                nc.vector.bn_stats(stat[:, k, c, :], src).then_inc(sem[name], 1)
                dve.wait_ge(sem[name], at(name, b, 2 * c + 1))
                own_wait(dve, b)
                nc.vector.bn_aggr(mv[:, k, c, :], stat[:, k, c, :]).then_inc(sem[name], 1)

            nc.vector.memset(qbd[:, :, :, :], 0.0).then_inc(c_ready, 1)
            nc.vector.memset(Am[:, :, :, :], 0.0).then_inc(c_ready, 1)

            def split(hi, lo, src, at):
                nc.vector.tensor_copy(hi, src).then_inc(c_split, 1)
                dve.wait_ge(c_split, at + 1)
                nc.vector.tensor_tensor(lo, src, hi.bitcast(F32), ALU.subtract).then_inc(c_split, 1)

            dve.wait_ge(c_w12, 1)
            split(WA[0][:, :, 2 * D:], WA[1][:, :, 2 * D:], PB[0][:, :].rearrange("p (k n) -> p k n", k=KT), 0)
            dve.wait_ge(c_in, 64 + 32)
            split(WA[0][:, :, 0:2 * D], WA[1][:, :, 0:2 * D],
                  raw[:, 0:KT * 2 * D].rearrange("p (k n) -> p k n", k=KT), 2)
            dve.wait_ge(c_in, 64 + 64)
            split(WB[0][:, :, :], WB[1][:, :, :], raw[:, :].rearrange("p (k n) -> p k n", k=KT), 4)
            dve.wait_ge(c_in, 64 + 80)
            split(WO[0][:, :, :], WO[1][:, :, :], raw[:, 0:VT * D].rearrange("p (k n) -> p k n", k=VT), 6)

            def run(s, j, e, B, C, A):
                p, n = s - 1, s + 1

                def lo_part(lo, hi, bank, hi_done, b, c, name):
                    dve.wait_ge(sem[hi_done], at(hi_done, b, c))
                    nc.vector.tensor_tensor(lo, bank, hi.bitcast(F32), ALU.subtract).then_inc(sem[name], 1)

                def copy_pairs(i, tl):
                    h = LV[i]
                    dve.wait_ge(sem["pe_lv"], at("pe_lv", s, 2 * i + tl + 1))
                    dst = Am[:, tl, :, :].rearrange("p a (n t h) -> p a n t h", t=2, h=h)[:, :, :, 1, :]
                    src = PL[tl][:, :].rearrange("p (a n h) -> p a n h", a=2 * NCH, h=h)
                    m = masks[:, i, :].bitcast(U32).rearrange("p (a n h) -> p a n h", a=1, h=h)
                    own_wait(dve, s)
                    nc.vector.copy_predicated(dst, m.to_broadcast([P, 2 * NCH, HC // h, h]), src)\
                        .then_inc(sem["dv_cp"], 1)

                def q_update(i, tl):
                    h = LV[i]
                    dve.wait_ge(sem["pe_lv"], at("pe_lv", s, 2 * i + tl + 1))
                    for hh in range(2):
                        r = slice(hh * HK, (hh + 1) * HK)
                        q = halves(qbd[r, tl, hh, :], h)[:, :, 1, :]
                        t = totals(h)[r, tl, :].rearrange("p (n t a) -> p n t a", t=2, a=1)[:, :, 0, :]
                        nc.vector.tensor_tensor(q, q, t.to_broadcast([HK, T // (2 * h), h]), ALU.mult)\
                            .then_inc(sem["dv_qu"], 1)

                def h_lo_part(m):
                    dve.wait_ge(sem["po_hhi"], at("po_hhi", p, m + 1))
                    nc.vector.tensor_tensor(h_lo[:, m, :], hf[:, m % 2, :], h_hi[:, m, :].bitcast(F32),
                                            ALU.subtract).then_inc(sem["dv_hlo"], 1)

                def o_part(c):
                    dve.wait_ge(sem["pe_att"], at("pe_att", s, c + 1))
                    if c:
                        dve.wait_ge(sem["pe_ogt"], at("pe_ogt", s, c))
                    else:
                        dve.wait_ge(sem["dv_dg"], at("dv_dg", s, 1))
                    for hd in range(H):
                        w = slice(hd * HV, (hd + 1) * HV)
                        nc.vector.scalar_tensor_tensor(o[:, w], v[:, c, w], dg[:, c * H + hd:c * H + hd + 1],
                                                       PO[:, w], ALU.mult, ALU.add).then_inc(sem["dv_o"], 1)

                def state(c):
                    dve.wait_ge(sem["pe_st"], at("pe_st", s, c + 1))
                    dve.wait_ge(sem["pe_att"], at("pe_att", s, c + 1))
                    if c:
                        dve.wait_ge(sem["dv_st"], at("dv_st", s, 4 * c))
                    for tl in range(KT):
                        for hh in range(2):
                            r = slice(hh * HK, (hh + 1) * HK)
                            w = slice(tl * 2 * HV + hh * HV, tl * 2 * HV + (hh + 1) * HV)
                            if c == 0:
                                ins = nc.vector.tensor_copy(S[r, tl, :], PS[r, w])
                            else:
                                t = totals(CH)[r, tl, c:c + 1]
                                ins = nc.vector.scalar_tensor_tensor(S[r, tl, :], S[r, tl, :], t, PS[r, w],
                                                                     ALU.mult, ALU.add)
                            ins.then_inc(sem["dv_st"], 1)

                def og(c):
                    dve.wait_ge(sem["po_ro"], at("po_ro", s, 2 * (c + 1)))
                    dve.wait_ge(sem["po_gw"], at("po_gw", s, c + 1))
                    for hd in range(H):
                        w = slice(hd * HV, (hd + 1) * HV)
                        nc.vector.scalar_tensor_tensor(o[:, w], o[:, w], rso[:, c * H + hd:c * H + hd + 1],
                                                       gs[:, c, w], ALU.mult, ALU.mult).then_inc(sem["dv_og"], 1)

                def og_lo(c):
                    lo_part(ogT_lo[:, :, :], ogT_hi[:, :, :],
                            PT[c % 2][:, :].rearrange("p (k t) -> p k t", k=VT), "ac_oghi", s, c + 1, "dv_oglo")

                def ln2(c):
                    dve.wait_ge(sem["ac_y"], at("ac_y", s, c + 1))
                    layer_stats(1, y[:, c, :], c, "dv_ln2", s)

                def gates(tl):
                    dve.wait_ge(sem["ac_abs"], at("ac_abs", n, tl + 1))
                    nc.vector.tensor_scalar(gm[:, tl, :], PB[tl][:, :], gkb[:, tl:tl + 1], 0.0,
                                            ALU.add, ALU.min).then_inc(sem["dv_gl"], 1)

                def gate_sub():
                    dve.wait_ge(sem["ac_l"], at("ac_l", n, 1))
                    dve.wait_ge(sem["dv_gl"], at("dv_gl", n, KT))
                    nc.vector.tensor_tensor(gm[:, :, :], gm[:, :, :], gn[:, :, :], ALU.subtract)\
                        .then_inc(sem["dv_gsub"], 1)

                def tots():
                    dve.wait_ge(sem["ac_a"], at("ac_a", n, 1))
                    for i, h in enumerate(LV):
                        if i:
                            dve.wait_ge(sem["dv_tot"], at("dv_tot", n, i))
                        t = totals(h).rearrange("p k (n t) -> p k n t", t=2)
                        nc.vector.tensor_tensor(totals(2 * h), t[:, :, :, 0], t[:, :, :, 1], ALU.mult)\
                            .then_inc(sem["dv_tot"], 1)

                def q_evac(tl):
                    dve.wait_ge(sem["pe_q"], at("pe_q", n, tl + 1))
                    dve.wait_ge(sem["ac_k"], at("ac_k", n, tl + 1))
                    nc.vector.tensor_tensor(qk[:, tl, :], PB[tl][:, :], kk[:, tl, :], ALU.mult)\
                        .then_inc(sem["dv_q"], 1)
                    dve.wait_ge(sem["ac_a"], at("ac_a", n, 1))
                    for hh in range(2):
                        r = slice(hh * HK, (hh + 1) * HK)
                        nc.vector.scalar_tensor_tensor(qbd[r, tl, hh, :], PB[tl][r, :], QSCALE, ga[r, tl, :],
                                                       ALU.mult, ALU.mult).then_inc(sem["dv_q"], 1)

                if B:
                    dve.wait_ge(sem["pe_diag"], at("pe_diag", s, 1))
                    nc.vector.tensor_copy(dg[:, :], PO[:, 0:NCH * H]).then_inc(sem["dv_dg"], 1)
                for step in range(2 * NL):
                    if B:
                        if step // 2 < MASKED:
                            copy_pairs(step // 2, step % 2)
                        q_update(step // 2, step % 2)
                    if C:
                        if step == 1:
                            dve.wait_ge(sem["po_x2"], at("po_x2", p, 1))
                            for c in range(NCH):
                                layer_stats(2, x2[:, c, :], c, "dv_ln3", p)
                        if step == 3:
                            for kt in range(KT):
                                lo_part(xT_lo[:, kt, :], xT_hi[:, kt, :], PT[kt][:, :], "ac_x3hi", p, kt + 1,
                                        "dv_x3lo")
                        if 5 <= step < 5 + FT:
                            h_lo_part(step - 5)
                    if A and step == 6:
                        dve.wait_ge(sem["x_in"], at("x_in", n, 16))
                        for c in range(NCH):
                            layer_stats(0, xb[1 - j][:, c, :], c, "dv_ln1", n)
                if C:
                    dve.wait_ge(sem["b_in"], at("b_in", e, 32))
                    for c in range(NCH):
                        dve.wait_ge(sem["pe_f2"], at("pe_f2", p, c + 1))
                        nc.vector.tensor_tensor(y[:, c, :], PB[c % 2][:, 0:D], b2s[:, :], ALU.add)\
                            .then_inc(sem["dv_y4"], 1)
                        dve.wait_ge(sem["dv_y4"], at("dv_y4", p, c + 1))
                        layer_stats(3, y[:, c, :], c, "dv_ln4", p)
                if A:
                    for kt in range(KT):
                        lo_part(xT_lo[:, kt, :], xT_hi[:, kt, :], PT[kt][:, :], "ac_xhi", n, kt + 1, "dv_xlo")
                    gates(0)
                    gates(1)
                if B:
                    o_part(0)
                    state(0)
                if A:
                    gate_sub()
                if B:
                    og(0)
                    state(1)
                if B:
                    og_lo(0)
                    o_part(1)
                    og(1)
                    state(2)
                    ln2(0)
                    og_lo(1)
                    o_part(2)
                    og(2)
                    ln2(1)
                    og_lo(2)
                    o_part(3)
                if A:
                    tots()
                    q_evac(0)
                if B:
                    og(3)
                    ln2(2)
                if A:
                    q_evac(1)
                if B:
                    og_lo(3)
                    ln2(3)

            program(dve, run)

        @block.scalar
        def _(act):
            def run(s, j, e, B, C, A):
                p, n = s - 1, s + 1

                def norm(k, dst, src, c, ready, name):
                    nc.scalar.activation(dst, src, ACT.Identity, bias=nm[:, k, c:c + 1],
                                         scale=rs[:, k, c:c + 1]).then_inc(sem[name], 1)

                def copy(dst, src, name):
                    nc.scalar.activation(dst, src, ACT.Copy).then_inc(sem[name], 1)

                def gelu(m):
                    act.wait_ge(sem["pe_f1"], at("pe_f1", p, m + 1))
                    if m >= 2:
                        act.wait_ge(sem["dv_hlo"], at("dv_hlo", p, m - 1))
                    nc.scalar.activation(hf[:, m % 2, :], PB[m % 2][:, :], ACT.Gelu_apprx_tanh,
                                         bias=b1s[:, m:m + 1]).then_inc(sem["ac_gelu"], 1)

                def copy_blocks(i, tl):
                    h = LV[i]
                    act.wait_ge(sem["pe_lv"], at("pe_lv", s, 2 * i + tl + 1))
                    for b in range(HC // h):
                        r = slice(2 * h * b, 2 * h * b + h)
                        copy(Am[r, tl, :, 2 * h * b + h:2 * h * (b + 1)],
                             PL[tl][r, :].rearrange("p (a n h) -> p a n h", a=2 * NCH, h=h)[:, :, b, :], "ac_cp")

                def squares(c):
                    act.wait_ge(sem["dv_o"], at("dv_o", s, H * (c + 1)))
                    for hd in range(H):
                        nc.scalar.activation(junk[:, hd * HV:(hd + 1) * HV], o[:, hd * HV:(hd + 1) * HV], ACT.Square,
                                             accum_out=ssq[:, c * H + hd:c * H + hd + 1]).then_inc(sem["ac_sq"], 1)

                def v_evac(c):
                    act.wait_ge(sem["pe_v"], at("pe_v", n, c + 1))
                    if B:
                        act.wait_ge(sem["dv_o"], at("dv_o", s, H * (c + 1)))
                    copy(v[:, c, :], PB[0][:, :], "ac_v")

                def g_evac(c):
                    act.wait_ge(sem["pe_g"], at("pe_g", n, c + 1))
                    if B:
                        act.wait_ge(sem["dv_og"], at("dv_og", s, H * (c + 1)))
                    nc.scalar.activation(gs[:, c, :], PB[1][:, :], ACT.Silu).then_inc(sem["ac_g"], 1)

                def og_hi(c):
                    act.wait_ge(sem["pe_ogt"], at("pe_ogt", s, c + 1))
                    if c:
                        act.wait_ge(sem["pe_wo"], at("pe_wo", s, c))
                    copy(ogT_hi[:, :, :], PT[c % 2][:, :].rearrange("p (k t) -> p k t", k=VT), "ac_oghi")

                def y_evac(c):
                    act.wait_ge(sem["pe_wo"], at("pe_wo", s, c + 1))
                    if c == 0 and C:
                        act.wait_ge(sem["st_out"], at("st_out", p, 16))
                    copy(y[:, c, :], PL[c % 2][:, 0:D], "ac_y")

                if C:
                    act.wait_ge(sem["po_ln2"], at("po_ln2", p, 4))
                    for c in range(NCH):
                        norm(1, y[:, c, :], y[:, c, :], c, "", "ac_t")
                    act.wait_ge(sem["po_ln3"], at("po_ln3", p, 4))
                    for c in range(NCH):
                        norm(2, xh[:, c, :], x2[:, c, :], c, "", "ac_xh3")
                    for kt in range(KT):
                        act.wait_ge(sem["pe_x3t"], at("pe_x3t", p, kt + 1))
                        copy(xT_hi[:, kt, :], PT[kt][:, :], "ac_x3hi")
                    act.wait_ge(sem["b_in"], at("b_in", e, 32))
                for step in range(4, 2 * NL):
                    if B and step // 2 >= MASKED:
                        copy_blocks(step // 2, step % 2)
                    if C and step < 4 + FT:
                        gelu(step - 4)
                if B:
                    for f in range(2):
                        act.wait_ge(sem["pe_kt"], at("pe_kt", s, f + 1))
                        copy(kT[:, 2 * f:2 * f + 2, :], PT[f][:, :].rearrange("p (c d) -> p c d", c=2), "ac_kt")
                if A:
                    for kt in range(KT):
                        act.wait_ge(sem["pe_xt"], at("pe_xt", n, kt + 1))
                        copy(xT_hi[:, kt, :], PT[kt][:, :], "ac_xhi")
                if A:
                    for tl in range(KT):
                        act.wait_ge(sem["pe_gl"], at("pe_gl", n, tl + 1))
                        nc.scalar.activation(gn[:, tl, :], PB[tl][:, :], ACT.Abs, bias=gkb[:, tl:tl + 1])\
                            .then_inc(sem["ac_abs"], 1)
                if C:
                    act.wait_ge(sem["po_ln4"], at("po_ln4", p, 4))
                    for c in range(NCH):
                        norm(3, y[:, c, :], y[:, c, :], c, "", "ac_fin")
                if A:
                    act.wait_ge(sem["ac_abs"], at("ac_abs", n, KT))
                    nc.scalar.activation(gn[:, :, :], gn[:, :, :], ACT.Exp, scale=-1.0).then_inc(sem["ac_e"], 1)
                    act.wait_ge(sem["ac_e"], at("ac_e", n, 1))
                    nc.scalar.activation(gn[:, :, :], gn[:, :, :], ACT.Ln, bias=1.0).then_inc(sem["ac_l"], 1)
                if B:
                    squares(0)
                if A:
                    for tl in range(KT):
                        act.wait_ge(sem["pe_k"], at("pe_k", n, tl + 1))
                        copy(kk[:, tl, :], PB[tl][:, :], "ac_k")
                    act.wait_ge(sem["dv_gsub"], at("dv_gsub", n, 1))
                    nc.scalar.activation(ga[:, :, :], gm[:, :, :], ACT.Exp, scale=1.0 / GATE_NORM)\
                        .then_inc(sem["ac_a"], 1)
                    v_evac(0)
                    g_evac(0)
                if B:
                    og_hi(0)
                    squares(1)
                if A:
                    v_evac(1)
                if B:
                    y_evac(0)
                if A:
                    g_evac(1)
                if B:
                    og_hi(1)
                    squares(2)
                if A:
                    v_evac(2)
                if B:
                    y_evac(1)
                if A:
                    g_evac(2)
                if B:
                    og_hi(2)
                    squares(3)
                    y_evac(2)
                    og_hi(3)
                if A:
                    v_evac(3)
                    g_evac(3)
                if B:
                    y_evac(3)

            program(act, run)

        @block.gpsimd
        def _(pool):
            nc.gpsimd.memset(ident[:, :], 1.0).then_inc(c_step, 1)
            nc.gpsimd.memset(masks[:, :, :], 1.0).then_inc(c_step, 1)
            nc.gpsimd.memset(ind[:, :], QSCALE).then_inc(c_step, 1)
            nc.gpsimd.memset(mhalf[:, :], -0.5).then_inc(c_step, 1)
            count = [4]

            def select(out, pattern, base, mult):
                pool.wait_ge(c_step, count[0])
                nc.gpsimd.affine_select(out=out, in_=out, compare_op=ALU.is_ge, fill=0.0, base=base,
                                        pattern=pattern, channel_multiplier=mult).then_inc(c_step, 1)
                count[0] += 1

            select(ident[:, :], [[1, P]], 0, -1)
            select(ident[:, :], [[-1, P]], 0, 1)
            select(ind[:, 0:1], [[0, 1]], HK - 1, -1)
            select(ind[:, 1:2], [[0, 1]], -HK, 1)
            for i in range(MASKED):
                h = LV[i]
                m = masks[:, i, :].rearrange("p (n h) -> p n h", h=h)
                select(m, [[-2 * h, HC // h], [0, h]], 0, 1)
                select(m, [[2 * h, HC // h], [0, h]], h - 1, -1)
            pool.wait_ge(c_step, count[0])
            nc.gpsimd.memset(ssq[:, :], 0.0).then_inc(c_ready, 1)
            pool.wait_ge(c_in, 64)

            def run(s, j, e, B, C, A):
                p, n = s - 1, s + 1

                def rstd(k, stats, b, name):
                    pool.wait_ge(sem[stats], at(stats, b, 2 * NCH))
                    own_wait(pool, b)
                    nc.gpsimd.tensor_scalar(rs[:, k, :], mv[:, k, :, 1], 1.0, EPS, ALU.mult, ALU.add)\
                        .then_inc(sem[name], 1)
                    pool.wait_ge(sem[name], at(name, b, 1))
                    nc.gpsimd.tensor_tensor(rs[:, k, :], rs[:, k, :], mhalf[:, 0:NCH], ALU.pow)\
                        .then_inc(sem[name], 1)
                    pool.wait_ge(sem[name], at(name, b, 2))
                    nc.gpsimd.tensor_tensor(nm[:, k, :], mv[:, k, :, 0], rs[:, k, :], ALU.mult)\
                        .then_inc(sem[name], 1)
                    pool.wait_ge(sem[name], at(name, b, 3))
                    own_wait(pool, b)
                    nc.gpsimd.tensor_scalar(nm[:, k, :], nm[:, k, :], -1.0, 0.0, ALU.mult, ALU.add)\
                        .then_inc(sem[name], 1)

                def k_update(i, tl):
                    h = LV[i]
                    pool.wait_ge(sem["pe_lv"], at("pe_lv", s, 2 * i + tl + 1))
                    k = halves(kk[:, tl, :], h)[:, :, 0, :]
                    t = totals(h)[:, tl, :].rearrange("p (n t a) -> p n t a", t=2, a=1)[:, :, 1, :]
                    nc.gpsimd.tensor_tensor(k, k, t.to_broadcast([P, T // (2 * h), h]), ALU.mult)\
                        .then_inc(sem["po_ku"], 1)

                def h_hi_part(m):
                    pool.wait_ge(sem["ac_gelu"], at("ac_gelu", p, m + 1))
                    own_wait(pool, s)
                    nc.gpsimd.tensor_copy(h_hi[:, m, :], hf[:, m % 2, :]).then_inc(sem["po_hhi"], 1)

                def o_rstd(c):
                    w = slice(c * H, (c + 1) * H)
                    pool.wait_ge(sem["ac_sq"], at("ac_sq", s, H * (c + 1)))
                    own_wait(pool, s)
                    nc.gpsimd.tensor_scalar(rso[:, w], ssq[:, w], 1.0 / HV, EPS, ALU.mult, ALU.add)\
                        .then_inc(sem["po_ro"], 1)
                    pool.wait_ge(sem["po_ro"], at("po_ro", s, 2 * c + 1))
                    nc.gpsimd.tensor_tensor(rso[:, w], rso[:, w], mhalf[:, w], ALU.pow)\
                        .then_inc(sem["po_ro"], 1)

                def gate_weight(c):
                    pool.wait_ge(sem["ac_g"], at("ac_g", n, c + 1))
                    nc.gpsimd.tensor_tensor(gs[:, c, :], gs[:, c, :], rmsb[:, :], ALU.mult)\
                        .then_inc(sem["po_gw"], 1)

                def split(c, en):
                    W, cols = (W1, DF) if c < 2 else (W2, D)
                    src = raw[:, :].rearrange("p (k n) -> p k n", n=cols)
                    if c % 2 == 0:
                        pool.wait_ge(sem["w_in"], at("w_in", en, 16 * (c // 2 + 1)))
                        if c == 0 and C:
                            pool.wait_ge(sem["pe_f1"], at("pe_f1", p, FT))
                        elif C:
                            pool.wait_ge(sem["pe_f2"], at("pe_f2", p, NCH))
                        own_wait(pool, s)
                        nc.gpsimd.tensor_copy(W[0][:, :, :], src).then_inc(sem["po_ws"], 1)
                    else:
                        pool.wait_ge(sem["po_ws"], at("po_ws", en, c))
                        nc.gpsimd.tensor_tensor(W[1][:, :, :], src, W[0][:, :, :].bitcast(F32), ALU.subtract)\
                            .then_inc(sem["po_ws"], 1)

                if C:
                    rstd(1, "dv_ln2", p, "po_ln2")
                for step in range(2 * NL):
                    if B:
                        k_update(step // 2, step % 2)
                    if C:
                        if step == 1:
                            pool.wait_ge(sem["ac_t"], at("ac_t", p, NCH))
                            nc.gpsimd.tensor_tensor(x2[:, :, :], y[:, :, :], xb[1 - j][:, :, :], ALU.add)\
                                .then_inc(sem["po_x2"], 1)
                            rstd(2, "dv_ln3", p, "po_ln3")
                        if 4 <= step < 4 + FT:
                            h_hi_part(step - 4)
                    if A and step == 8:
                        rstd(0, "dv_ln1", n, "po_ln1")
                        pool.wait_ge(sem["po_ln1"], at("po_ln1", n, 4))
                        if C:
                            pool.wait_ge(sem["pe_x3t"], at("pe_x3t", p, KT))
                        for c in range(NCH):
                            own_wait(pool, n)
                            nc.gpsimd.tensor_scalar(xh[:, c, :], xb[1 - j][:, c, :], rs[:, 0, c:c + 1],
                                                    nm[:, 0, c:c + 1], ALU.mult, ALU.add).then_inc(sem["po_xh"], 1)
                if C:
                    rstd(3, "dv_ln4", p, "po_ln4")
                    pool.wait_ge(sem["ac_fin"], at("ac_fin", p, NCH))
                    nc.gpsimd.tensor_tensor(y[:, :, :], y[:, :, :], x2[:, :, :], ALU.add)\
                        .then_inc(sem["po_fin"], 1)
                for c in range(NCH):
                    if B:
                        o_rstd(c)
                        if A and j == 0:
                            split(c, 0 if isinstance(s, int) else e + 1)
                    if A:
                        gate_weight(c)

            program(pool, run)


_IN = ["L0_attn_x", "L0_attn_Wq", "L0_attn_Wk", "L0_attn_Wv", "L0_attn_Wg", "L0_attn_gk_w1", "L0_attn_gk_w2",
       "L0_attn_gk_b", "L0_attn_Wo", "L0_attn_rms_w", "L0_ffn_w1", "L0_ffn_b1", "L0_ffn_w2", "L0_ffn_b2"]


def kernel(**inputs):
    import numpy as np
    import concourse.bacc as bacc
    from concourse import mybir
    from concourse.bass_utils import run_bass_kernel_spmd

    a = {n: np.asarray(inputs[n]) for n in _IN}
    P, H = 128, 4
    a["L0_attn_gk_w1"] = a["L0_attn_gk_w1"].T
    a["L0_attn_gk_b"] = a["L0_attn_gk_b"].reshape(-1, P).T
    a["L0_attn_rms_w"] = np.tile(a["L0_attn_rms_w"], (P, H))
    E = a["L0_ffn_b1"].shape[0]
    a["L0_ffn_b1"] = a["L0_ffn_b1"].reshape(E, -1, P).transpose(0, 2, 1)
    a["L0_ffn_b2"] = np.repeat(a["L0_ffn_b2"][:, None, :], P, axis=1)

    nc = bacc.Bacc("TRN2", target_bir_lowering=False, num_devices=1)
    arrays, args = {}, []
    for n in _IN:
        arrays[n] = np.ascontiguousarray(a[n])
        args.append(nc.dram_tensor(n, arrays[n].shape, mybir.dt.from_np(arrays[n].dtype), kind="ExternalInput").ap())
    shape = arrays["L0_attn_x"].shape
    args.append(nc.dram_tensor("out", shape, mybir.dt.float32, kind="ExternalOutput").ap())
    build(nc, *args)
    r = run_bass_kernel_spmd(nc, [arrays], core_ids=[0])
    return r.results[0]["out"]
```

```python
def build(nc, x_d, wq_d, wk_d, wv_d, wg_d, w1t_d, w2g_d, gkb_d, wo_d, rms_d,
          fw1_d, fb1_d, fw2_d, fb2_d, out_d):
    from contextlib import ExitStack
    from concourse import mybir

    F32, F32R, U32 = mybir.dt.float32, mybir.dt.float32r, mybir.dt.uint32
    ACT, ALU = mybir.ActivationFunctionType, mybir.AluOpType
    P = 128
    NB, T, D = x_d.shape
    E, _, DF = fw1_d.shape
    LR = w2g_d.shape[0]
    DV = wv_d.shape[1]
    H = 4
    HV = DV // H
    HK = D // H
    CH = 128
    NCH = T // CH
    KT = D // P
    FT = DF // P
    VT = DV // P
    LV = [1, 2, 4, 8, 16, 32, 64]
    NL = len(LV)
    MASKED = 5
    HC = CH // 2
    EPS = 1e-5
    QSCALE = HK ** -0.5
    GATE_NORM = 16.0
    SLOTS = NB

    ctx = ExitStack()
    with ctx:
        def sb(name, shape, dt=F32):
            return ctx.enter_context(nc.sbuf_tensor(name, shape, dt))

        def ps(name):
            return ctx.enter_context(nc.psum_tensor(name, [P, 512], F32))

        xb = [sb(f"x_in{j}", [P, NCH, D]) for j in range(2)]
        xh = sb("x_normed", [P, NCH, D])
        xT_hi, xT_lo = sb("xT_hi", [P, KT, T], F32R), sb("xT_lo", [P, KT, T], F32R)
        x2 = sb("x_mid", [P, NCH, D])
        y = sb("y", [P, NCH, D])
        qbd = sb("q_blockdiag", [P, KT, 2, T])
        kk = sb("k_decayed", [P, KT, T])
        ga = sb("gates", [P, KT, T])
        qk = sb("q_times_k", [P, KT, T])
        gn = qk
        tot = sb("block_totals", [P, KT, T])
        Am = sb("attn_T", [P, KT, NCH * 2, CH])
        kT = sb("k_tokens", [P, NCH, D])
        S = sb("state", [P, KT, HV])
        v = sb("v", [P, NCH, DV])
        gs = sb("out_gate", [P, NCH, DV])
        o = sb("o", [P, 2, DV])
        ogT_hi, ogT_lo = sb("ogT_hi", [P, VT, CH], F32R), sb("ogT_lo", [P, VT, CH], F32R)
        hf = sb("gelu_out", [P, 2, T])
        gm = hf
        h_hi, h_lo = sb("h_hi", [P, FT, T], F32R), sb("h_lo", [P, FT, T], F32R)
        NA = 3 * D
        WA = [sb(f"w_qkg_{n}", [P, KT, NA], F32R) for n in ("hi", "lo")]
        WB = [sb(f"w_vg_{n}", [P, KT, 2 * DV], F32R) for n in ("hi", "lo")]
        WO = [sb(f"w_o_{n}", [P, VT, D], F32R) for n in ("hi", "lo")]
        W1 = [sb(f"w_ff1_{n}", [P, KT, DF], F32R) for n in ("hi", "lo")]
        W2 = [sb(f"w_ff2_{n}", [P, FT, D], F32R) for n in ("hi", "lo")]
        RAW = KT * DF
        raw = sb("w_raw", [P, RAW])
        masks = sb("level_masks", [P, MASKED, HC])
        rmsb = sb("rms_w_rows", [P, DV])
        b2s = sb("ff_b2_rows", [P, D])
        b1s = sb("ff_b1_cols", [P, FT])
        gkb = sb("gk_b_cols", [P, KT])
        ident = sb("ident", [P, P])
        ind = sb("head_sum", [P, 2])
        mhalf = sb("minus_half", [P, NCH * H])
        stat = sb("bn", [P, 4, NCH, 6])
        mv = sb("mean_var", [P, 4, NCH, 2])
        rs = sb("rstd", [P, 4, NCH])
        nm = sb("minus_mean_rstd", [P, 4, NCH])
        ssq = sb("o_sumsq", [P, NCH * H])
        rso = sb("o_rstd", [P, NCH * H])
        dg = sb("qk_diag", [P, NCH * H])
        junk = sb("square_out", [P, DV], mybir.dt.bfloat16)
        w1t = raw[0:LR, 0:D]
        w2g = raw[0:LR, D:2 * D]

        PB = [ps(f"ps_big{j}") for j in range(2)]
        PT = [ps(f"ps_transpose{j}") for j in range(2)]
        PL = [ps(f"ps_level{j}") for j in range(2)]
        PO, PS = ps("ps_out"), ps("ps_state")

        toff, at = {}, 0
        for h in LV[1:] + [CH]:
            toff[h] = at
            at += T // h

        def totals(h):
            return ga[:, :, :] if h == 1 else tot[:, :, toff[h]:toff[h] + T // h]

        PER = dict(
            x_in=16, st_out=16, w_in=32, b_in=32,
            pe_diag=1, pe_lv=2 * NL, pe_x3t=KT, pe_f1=FT, pe_f2=NCH, pe_kt=2, pe_xt=KT, pe_gl=KT,
            pe_k=KT, pe_q=KT, pe_v=NCH, pe_g=NCH, pe_st=NCH - 1, pe_att=NCH, pe_ogt=NCH, pe_wo=NCH,
            dv_dg=1, dv_ln1=2 * NCH + 1, dv_ln2=3 * NCH, dv_ln3=3 * NCH, dv_ln4=3 * NCH, dv_x3lo=KT,
            dv_t=NCH, dv_x2=NCH, dv_xh=NCH, dv_t4=NCH, dv_xh3=NCH,
            dv_cp=2 * MASKED, dv_qu=4 * NL, dv_hlo=FT, dv_y4=NCH, dv_xlo=KT, dv_gl=KT, dv_gsub=1,
            dv_q=3 * KT, dv_st=4 * (NCH - 1), dv_o=NCH * H, dv_og=NCH * H, dv_oglo=NCH,
            ac_x3hi=KT, ac_gelu=FT, ac_hhi=FT, ac_ws=2, ac_cp=6, ac_kt=2, ac_xhi=KT,
            ac_abs=KT, ac_e=1, ac_l=1, ac_a=1, ac_k=KT, ac_v=NCH, ac_g=NCH, ac_sq=NCH * H, ac_oghi=NCH, ac_y=NCH,
            po_p1=1, po_p2=NCH, po_p3=NCH, po_p4=NCH, po_ku=2 * NL, po_fin=NCH, po_tot=NL,
            po_gw=NCH, po_ro=2 * NCH, po_w1=4, po_w2=4,
        )
        sem = {n: ctx.enter_context(nc.semaphore(n)) for n in PER}
        c_in = ctx.enter_context(nc.semaphore("const_in"))
        c_ready = ctx.enter_context(nc.semaphore("const_ready"))
        c_step = ctx.enter_context(nc.semaphore("const_step"))
        c_split = ctx.enter_context(nc.semaphore("const_split"))
        c_w12 = ctx.enter_context(nc.semaphore("const_w12"))

        def at(name, b, c):
            return b * PER[name] + c

        def own_wait(eng, b):
            if not isinstance(b, int):
                eng.nop(nofuse=True)

        def program(eng, run):
            run(-1, 1, 0, False, False, True)
            run(0, 0, 0, True, False, True)
            with eng.Fori(0, NB // 2 - 1) as i:
                run(i * 2 + 1, 1, i, True, True, True)
                run(i * 2 + 2, 0, i, True, True, True)
            run(NB - 1, 1, E - 1, True, True, False)
            run(NB, 0, E - 1, False, True, False)

        def halves(ap, h):
            return ap.rearrange("p (n t h) -> p n t h", t=2, h=h)

        block = ctx.enter_context(nc.Block())

        @block.sync
        def _(sp):
            sp.dma_start(gkb[:, :], gkb_d).then_inc(c_in, 16)
            sp.dma_start(rmsb[:, :], rms_d).then_inc(c_in, 16)
            sp.dma_start(w1t, w1t_d).then_inc(c_in, 16)
            sp.dma_start(w2g, w2g_d).then_inc(c_in, 16)
            sp.dma_start(xb[0][:, :, :], x_d[0].rearrange("(c p) d -> p c d", p=P)).then_inc(sem["x_in"], 16)
            parts = [(raw[:, 0:KT * 2 * D].rearrange("p (k n) -> p k n", k=KT), [wq_d, wk_d]),
                     (raw[:, 0:KT * 2 * DV].rearrange("p (k n) -> p k n", k=KT)[:, :, 0:2 * DV], [wv_d, wg_d]),
                     (raw[:, 0:VT * D].rearrange("p (k n) -> p k n", k=VT), [wo_d])]
            for n, (dst, srcs) in enumerate(parts):
                sp.wait_ge(c_split, 2 * n + 2)
                w = srcs[0].shape[1]
                for m, src in enumerate(srcs):
                    sp.dma_start(dst[:, :, m * w:(m + 1) * w],
                                 src.rearrange("(k p) n -> p k n", p=P)).then_inc(c_in, 16)

            def load_w1(e, s, C):
                sp.dma_start(raw[:, :].rearrange("p (k n) -> p k n", k=KT),
                             fw1_d[e].rearrange("(k p) n -> p k n", p=P)).then_inc(sem["w_in"], 16)
                if C:
                    sp.wait_ge(sem["ac_gelu"], at("ac_gelu", s - 1, FT))
                    sp.wait_ge(sem["dv_y4"], at("dv_y4", s - 1, NCH))
                sp.dma_start(b1s[:, :], fb1_d[e]).then_inc(sem["b_in"], 16)
                sp.dma_start(b2s[:, :], fb2_d[e]).then_inc(sem["b_in"], 16)

            def load_w2(e):
                sp.wait_ge(sem["po_w1"], at("po_w1", e, 4))
                sp.dma_start(raw[:, :].rearrange("p (k n) -> p k n", k=FT),
                             fw2_d[e].rearrange("(k p) n -> p k n", p=P)).then_inc(sem["w_in"], 16)

            def run(s, j, e, B, C, A):
                if B and A:
                    if C:
                        sp.wait_ge(sem["dv_x2"], at("dv_x2", s - 1, NCH))
                    sp.dma_start(xb[1 - j][:, :, :],
                                 x_d[s + 1].rearrange("(c p) d -> p c d", p=P)).then_inc(sem["x_in"], 16)
                if B and A and j == 0:
                    if isinstance(s, int):
                        sp.wait_ge(c_split, 8)
                        load_w1(0, s, C)
                    else:
                        sp.wait_ge(sem["po_w2"], at("po_w2", e, 4))
                        load_w1(e + 1, s, C)
                if C:
                    sp.wait_ge(sem["po_fin"], at("po_fin", s - 1, NCH))
                    sp.dma_start(out_d[s - 1].rearrange("(c p) d -> p c d", p=P),
                                 y[:, :, :]).then_inc(sem["st_out"], 16)
                if B and A and j == 0:
                    load_w2(0 if isinstance(s, int) else e + 1)

            program(sp, run)
            sp.wait_ge(sem["st_out"], 16 * NB)

        @block.tensor
        def _(pe):
            def three(out, lhs, rhs):
                n = len(lhs)
                for i in range(n):
                    (ah, al), (bh, bl) = lhs[i], rhs[i]
                    nc.tensor.matmul(out, ah, bh, start=(i == 0), stop=False)
                    nc.tensor.matmul(out, ah, bl, start=False, stop=False)
                    last = nc.tensor.matmul(out, al, bh, start=False, stop=(i == n - 1))
                return last

            pe.wait_ge(c_ready, 3)
            pe.wait_ge(c_in, 64)
            for kt in range(KT):
                last = nc.tensor.matmul(PB[0][:, kt * D:(kt + 1) * D], w1t[:, kt * P:(kt + 1) * P],
                                        w2g, start=True, stop=True)
            last.then_inc(c_w12, 1)
            pe.wait_ge(c_split, 8)

            def transpose_tokens(src, kt):
                for c in range(NCH):
                    last = nc.tensor.transpose(PT[kt][:, c * P:(c + 1) * P],
                                               src[:, c, kt * P:(kt + 1) * P], ident[:, :])
                return last

            def run(s, j, e, B, C, A):
                p, n = s - 1, s + 1

                def level(i, tl):
                    h = LV[i]
                    if i == 0:
                        if tl == 0:
                            pe.wait_ge(sem["dv_q"], at("dv_q", s, 3 * KT))
                            pe.wait_ge(sem["ac_k"], at("ac_k", s, KT))
                        if C:
                            pe.wait_ge(sem["ac_y"], at("ac_y", p, 3 + tl))
                    else:
                        pe.wait_ge(sem["dv_qu"], at("dv_qu", s, 4 * (i - 1) + 2 * tl + 2))
                        pe.wait_ge(sem["po_ku"], at("po_ku", s, 2 * (i - 1) + tl + 1))
                        if i - 1 < MASKED:
                            pe.wait_ge(sem["dv_cp"], at("dv_cp", s, 2 * (i - 1) + tl + 1))
                        else:
                            pe.wait_ge(sem["ac_cp"], at("ac_cp", s, 2 * tl + 2))
                    for c in range(NCH):
                        q = qbd[:, tl, :, c * CH:(c + 1) * CH].rearrange("p a (n t h) -> p a n t h", t=2, h=h)
                        last = nc.tensor.matmul(PL[tl][:, c * CH:(c + 1) * CH],
                                                kk[:, tl, c * CH:(c + 1) * CH], q[:, :, :, 1, :],
                                                start=True, stop=True)
                    last.then_inc(sem["pe_lv"], 1)

                def diag():
                    pe.wait_ge(sem["dv_q"], at("dv_q", s, 3 * KT))
                    if C:
                        pe.wait_ge(sem["dv_o"], at("dv_o", p, NCH * H))
                    for c in range(NCH):
                        for tl in range(KT):
                            w = c * H + 2 * tl
                            last = nc.tensor.matmul(PO[:, w:w + 2], qk[:, tl, c * CH:(c + 1) * CH],
                                                    ind[:, :], start=True, stop=True)
                    last.then_inc(sem["pe_diag"], 1)

                def x3t(kt):
                    pe.wait_ge(sem["dv_xh3"], at("dv_xh3", p, NCH))
                    pe.wait_ge(sem["dv_oglo"], at("dv_oglo", p, 3 + kt))
                    transpose_tokens(xh, kt).then_inc(sem["pe_x3t"], 1)

                def f1(m):
                    pe.wait_ge(sem["dv_x3lo"], at("dv_x3lo", p, KT))
                    pe.wait_ge(sem["po_w1"], at("po_w1", e, 4))
                    if m >= 2:
                        pe.wait_ge(sem["ac_gelu"], at("ac_gelu", p, m - 1))
                    elif B and m == 0:
                        pe.wait_ge(sem["ac_v"], at("ac_v", s, NCH))
                    elif B:
                        pe.wait_ge(sem["ac_g"], at("ac_g", s, NCH))
                    w = slice(m * P, (m + 1) * P)
                    three(PB[m % 2][:, :], [(W1[0][:, kt, w], W1[1][:, kt, w]) for kt in range(KT)],
                          [(xT_hi[:, kt, :], xT_lo[:, kt, :]) for kt in range(KT)]).then_inc(sem["pe_f1"], 1)

                def f2(c):
                    pe.wait_ge(sem["dv_hlo"], at("dv_hlo", p, FT))
                    pe.wait_ge(sem["po_w2"], at("po_w2", e, 4))
                    if c >= 2:
                        pe.wait_ge(sem["dv_y4"], at("dv_y4", p, c - 1))
                    else:
                        pe.wait_ge(sem["ac_gelu"], at("ac_gelu", p, FT - 1 + c))
                    t = slice(c * CH, (c + 1) * CH)
                    three(PB[c % 2][:, 0:D], [(h_hi[:, m, t], h_lo[:, m, t]) for m in range(FT)],
                          [(W2[0][:, m, :], W2[1][:, m, :]) for m in range(FT)]).then_inc(sem["pe_f2"], 1)

                def kh(f):
                    pe.wait_ge(sem["po_ku"], at("po_ku", s, 2 * NL))
                    if A:
                        pe.wait_ge(sem["dv_xlo"], at("dv_xlo", n, f + 1))
                    elif C:
                        pe.wait_ge(sem["dv_x3lo"], at("dv_x3lo", p, f + 1))
                    for c in range(2):
                        for tl in range(KT):
                            w = (2 * f + c) * CH
                            last = nc.tensor.transpose(PT[f][:, c * D + tl * P:c * D + (tl + 1) * P],
                                                       kk[:, tl, w:w + CH], ident[:, :])
                    last.then_inc(sem["pe_kt"], 1)

                def xt(kt):
                    pe.wait_ge(sem["dv_xh"], at("dv_xh", n, NCH))
                    if C:
                        pe.wait_ge(sem["dv_x3lo"], at("dv_x3lo", p, kt + 1))
                    elif B:
                        pe.wait_ge(sem["dv_xlo"], at("dv_xlo", s, kt + 1))
                    transpose_tokens(xh, kt).then_inc(sem["pe_xt"], 1)

                def feature_tile(bank, col):
                    w = slice(col, col + P)
                    return three(bank[:, :], [(WA[0][:, kt, w], WA[1][:, kt, w]) for kt in range(KT)],
                                 [(xT_hi[:, kt, :], xT_lo[:, kt, :]) for kt in range(KT)])

                def token_tile(bank, c, half):
                    t, w = slice(c * CH, (c + 1) * CH), slice(half * DV, (half + 1) * DV)
                    return three(bank[:, :], [(xT_hi[:, kt, t], xT_lo[:, kt, t]) for kt in range(KT)],
                                 [(WB[0][:, kt, w], WB[1][:, kt, w]) for kt in range(KT)])

                def gl(tl):
                    pe.wait_ge(sem["dv_xlo"], at("dv_xlo", n, KT))
                    if C:
                        pe.wait_ge(sem["dv_y4"], at("dv_y4", p, 3 + tl))
                    elif B:
                        pe.wait_ge(sem[("ac_v", "ac_g")[tl]], at(("ac_v", "ac_g")[tl], s, NCH))
                    feature_tile(PB[tl], 2 * D + tl * P).then_inc(sem["pe_gl"], 1)

                def kp(tl):
                    pe.wait_ge(sem["dv_gl"], at("dv_gl", n, tl + 1))
                    feature_tile(PB[tl], D + tl * P).then_inc(sem["pe_k"], 1)

                def qp(tl):
                    pe.wait_ge(sem[("ac_v", "ac_g")[tl]], at(("ac_v", "ac_g")[tl], n, 2))
                    feature_tile(PB[tl], tl * P).then_inc(sem["pe_q"], 1)

                def vp(c):
                    if c == 0:
                        pe.wait_ge(sem["ac_k"], at("ac_k", n, 1))
                    elif c == 2:
                        pe.wait_ge(sem["dv_q"], at("dv_q", n, 3))
                    else:
                        pe.wait_ge(sem["ac_v"], at("ac_v", n, c))
                    token_tile(PB[0], c, 0).then_inc(sem["pe_v"], 1)

                def gp(c):
                    if c == 0:
                        pe.wait_ge(sem["ac_k"], at("ac_k", n, 2))
                    elif c == 2:
                        pe.wait_ge(sem["dv_q"], at("dv_q", n, 6))
                    else:
                        pe.wait_ge(sem["ac_g"], at("ac_g", n, c))
                    token_tile(PB[1], c, 1).then_inc(sem["pe_g"], 1)

                def st(c):
                    pe.wait_ge(sem["ac_kt"], at("ac_kt", s, c // 2 + 1))
                    pe.wait_ge(sem["ac_v"], at("ac_v", s, c + 1))
                    if c:
                        pe.wait_ge(sem["dv_st"], at("dv_st", s, 4 * c))
                    elif C:
                        pe.wait_ge(sem["dv_st"], at("dv_st", p, 4 * (NCH - 1)))
                    for tl in range(KT):
                        last = nc.tensor.matmul(PS[:, tl * 2 * HV:(tl + 1) * 2 * HV],
                                                kT[:, c, tl * P:(tl + 1) * P],
                                                v[:, c, tl * 2 * HV:(tl + 1) * 2 * HV], start=True, stop=True)
                    last.then_inc(sem["pe_st"], 1)

                def att(c):
                    pe.wait_ge(sem["dv_cp"], at("dv_cp", s, 2 * MASKED))
                    pe.wait_ge(sem["ac_cp"], at("ac_cp", s, 6))
                    pe.wait_ge(sem["dv_qu"], at("dv_qu", s, 4 * NL))
                    pe.wait_ge(sem["ac_v"], at("ac_v", s, c + 1))
                    if c:
                        pe.wait_ge(sem["dv_o"], at("dv_o", s, c * H))
                        pe.wait_ge(sem["dv_st"], at("dv_st", s, 4 * c))
                    else:
                        pe.wait_ge(sem["dv_dg"], at("dv_dg", s, 1))
                    for hd in range(H):
                        tl, hh = hd // 2, hd % 2
                        w = slice(hd * HV, (hd + 1) * HV)
                        last = nc.tensor.matmul(PO[:, w], Am[:, tl, 2 * c + hh, :], v[:, c, w],
                                                start=True, stop=(c == 0))
                        if c:
                            last = nc.tensor.matmul(PO[:, w], qbd[:, tl, hh, c * CH:(c + 1) * CH],
                                                    S[:, tl, :], start=False, stop=True)
                    last.then_inc(sem["pe_att"], 1)

                def ogt(c):
                    pe.wait_ge(sem["dv_og"], at("dv_og", s, H * (c + 1)))
                    if c >= 2:
                        pe.wait_ge(sem["dv_oglo"], at("dv_oglo", s, c - 1))
                    else:
                        pe.wait_ge(sem["ac_kt"], at("ac_kt", s, c + 1))
                    for k in range(VT):
                        last = nc.tensor.transpose(PT[c % 2][:, k * P:(k + 1) * P], o[:, c % 2, k * P:(k + 1) * P], ident[:, :])
                    last.then_inc(sem["pe_ogt"], 1)

                def wo(c):
                    pe.wait_ge(sem["dv_oglo"], at("dv_oglo", s, c + 1))
                    if c >= 2:
                        pe.wait_ge(sem["ac_y"], at("ac_y", s, c - 1))
                    else:
                        pe.wait_ge(sem["ac_cp"], at("ac_cp", s, 5 + c))
                    three(PL[c % 2][:, 0:D], [(ogT_hi[:, k, :], ogT_lo[:, k, :]) for k in range(VT)],
                          [(WO[0][:, k, :], WO[1][:, k, :]) for k in range(VT)]).then_inc(sem["pe_wo"], 1)

                if B:
                    diag()
                for step in range(2 * NL):
                    if B:
                        level(step // 2, step % 2)
                    if C:
                        if step == 1:
                            x3t(0)
                            x3t(1)
                        if 2 <= step < 2 + FT:
                            f1(step - 2)
                        if 11 <= step < 14:
                            f2(step - 11)
                if A:
                    xt(0)
                    xt(1)
                if C:
                    f2(3)
                if B:
                    kh(0)
                    kh(1)
                if A:
                    gl(0)
                    gl(1)
                if B:
                    st(0)
                    att(0)
                if A:
                    kp(0)
                    kp(1)
                if B:
                    st(1)
                    att(1)
                if A:
                    vp(0)
                    gp(0)
                if B:
                    st(2)
                    att(2)
                    ogt(0)
                if A:
                    vp(1)
                if B:
                    wo(0)
                    att(3)
                    ogt(1)
                if A:
                    gp(1)
                    qp(0)
                if B:
                    wo(1)
                    ogt(2)
                if A:
                    qp(1)
                    vp(2)
                if B:
                    wo(2)
                    ogt(3)
                if A:
                    gp(2)
                if B:
                    wo(3)
                if A:
                    vp(3)
                    gp(3)

            program(pe, run)

        @block.vector
        def _(dve):
            nc.vector.memset(qbd[:, :, :, :], 0.0).then_inc(c_ready, 1)
            nc.vector.memset(Am[:, :, :, :], 0.0).then_inc(c_ready, 1)

            def split(hi, lo, src, at):
                nc.vector.tensor_copy(hi, src).then_inc(c_split, 1)
                dve.wait_ge(c_split, at + 1)
                nc.vector.tensor_tensor(lo, src, hi.bitcast(F32), ALU.subtract).then_inc(c_split, 1)

            dve.wait_ge(c_w12, 1)
            split(WA[0][:, :, 2 * D:], WA[1][:, :, 2 * D:], PB[0][:, :].rearrange("p (k n) -> p k n", k=KT), 0)
            dve.wait_ge(c_in, 64 + 32)
            split(WA[0][:, :, 0:2 * D], WA[1][:, :, 0:2 * D],
                  raw[:, 0:KT * 2 * D].rearrange("p (k n) -> p k n", k=KT), 2)
            dve.wait_ge(c_in, 64 + 64)
            split(WB[0][:, :, :], WB[1][:, :, :], raw[:, :].rearrange("p (k n) -> p k n", k=KT), 4)
            dve.wait_ge(c_in, 64 + 80)
            split(WO[0][:, :, :], WO[1][:, :, :], raw[:, 0:VT * D].rearrange("p (k n) -> p k n", k=VT), 6)

            def run(s, j, e, B, C, A):
                p, n = s - 1, s + 1

                def lo_part(lo, hi, bank, hi_done, b, c, name):
                    dve.wait_ge(sem[hi_done], at(hi_done, b, c))
                    nc.vector.tensor_tensor(lo, bank, hi.bitcast(F32), ALU.subtract).then_inc(sem[name], 1)

                def copy_pairs(i, tl):
                    h = LV[i]
                    dve.wait_ge(sem["pe_lv"], at("pe_lv", s, 2 * i + tl + 1))
                    dst = Am[:, tl, :, :].rearrange("p a (n t h) -> p a n t h", t=2, h=h)[:, :, :, 1, :]
                    src = PL[tl][:, :].rearrange("p (a n h) -> p a n h", a=2 * NCH, h=h)
                    m = masks[:, i, :].bitcast(U32).rearrange("p (a n h) -> p a n h", a=1, h=h)
                    own_wait(dve, s)
                    nc.vector.copy_predicated(dst, m.to_broadcast([P, 2 * NCH, HC // h, h]), src)\
                        .then_inc(sem["dv_cp"], 1)

                def q_update(i, tl):
                    h = LV[i]
                    dve.wait_ge(sem["pe_lv"], at("pe_lv", s, 2 * i + tl + 1))
                    dve.wait_ge(sem["po_tot"], at("po_tot", s, NL))
                    for hh in range(2):
                        r = slice(hh * HK, (hh + 1) * HK)
                        q = halves(qbd[r, tl, hh, :], h)[:, :, 1, :]
                        t = totals(h)[r, tl, :].rearrange("p (n t a) -> p n t a", t=2, a=1)[:, :, 0, :]
                        nc.vector.tensor_tensor(q, q, t.to_broadcast([HK, T // (2 * h), h]), ALU.mult)\
                            .then_inc(sem["dv_qu"], 1)

                def h_lo_part(m):
                    dve.wait_ge(sem["ac_hhi"], at("ac_hhi", p, m + 1))
                    nc.vector.tensor_tensor(h_lo[:, m, :], hf[:, m % 2, :], h_hi[:, m, :].bitcast(F32),
                                            ALU.subtract).then_inc(sem["dv_hlo"], 1)

                def o_part(c):
                    dve.wait_ge(sem["pe_att"], at("pe_att", s, c + 1))
                    if c >= 2:
                        dve.wait_ge(sem["pe_ogt"], at("pe_ogt", s, c - 1))
                    elif c == 0:
                        dve.wait_ge(sem["dv_dg"], at("dv_dg", s, 1))
                    for hd in range(H):
                        w = slice(hd * HV, (hd + 1) * HV)
                        nc.vector.scalar_tensor_tensor(o[:, c % 2, w], v[:, c, w], dg[:, c * H + hd:c * H + hd + 1],
                                                       PO[:, w], ALU.mult, ALU.add).then_inc(sem["dv_o"], 1)

                def state(c):
                    dve.wait_ge(sem["pe_st"], at("pe_st", s, c + 1))
                    dve.wait_ge(sem["pe_att"], at("pe_att", s, c + 1))
                    if c:
                        dve.wait_ge(sem["dv_st"], at("dv_st", s, 4 * c))
                    for tl in range(KT):
                        for hh in range(2):
                            r = slice(hh * HK, (hh + 1) * HK)
                            w = slice(tl * 2 * HV + hh * HV, tl * 2 * HV + (hh + 1) * HV)
                            if c == 0:
                                ins = nc.vector.tensor_copy(S[r, tl, :], PS[r, w])
                            else:
                                t = totals(CH)[r, tl, c:c + 1]
                                ins = nc.vector.scalar_tensor_tensor(S[r, tl, :], S[r, tl, :], t, PS[r, w],
                                                                     ALU.mult, ALU.add)
                            ins.then_inc(sem["dv_st"], 1)

                def og(c):
                    dve.wait_ge(sem["po_ro"], at("po_ro", s, 2 * (c + 1)))
                    dve.wait_ge(sem["po_gw"], at("po_gw", s, c + 1))
                    for hd in range(H):
                        w = slice(hd * HV, (hd + 1) * HV)
                        nc.vector.scalar_tensor_tensor(o[:, c % 2, w], o[:, c % 2, w], rso[:, c * H + hd:c * H + hd + 1],
                                                       gs[:, c, w], ALU.mult, ALU.mult).then_inc(sem["dv_og"], 1)

                def og_lo(c):
                    lo_part(ogT_lo[:, :, :], ogT_hi[:, :, :],
                            PT[c % 2][:, :].rearrange("p (k t) -> p k t", k=VT), "ac_oghi", s, c + 1, "dv_oglo")

                def stats_eps(k, src, c, name, b):
                    nc.vector.bn_stats(stat[:, k, c, :], src).then_inc(sem[name], 1)
                    dve.wait_ge(sem[name], at(name, b, 3 * c + 1))
                    own_wait(dve, b)
                    nc.vector.bn_aggr(mv[:, k, c, :], stat[:, k, c, :]).then_inc(sem[name], 1)
                    dve.wait_ge(sem[name], at(name, b, 3 * c + 2))
                    nc.vector.tensor_scalar(rs[:, k, c:c + 1], mv[:, k, c, 1:2], EPS, None, ALU.add)\
                        .then_inc(sem[name], 1)

                def ln1_stats():
                    dve.wait_ge(sem["x_in"], at("x_in", n, 16))
                    for c in range(NCH):
                        nc.vector.bn_stats(stat[:, 0, c, :], xb[1 - j][:, c, :]).then_inc(sem["dv_ln1"], 1)

                def ln1_aggregate():
                    dve.wait_ge(sem["dv_ln1"], at("dv_ln1", n, NCH))
                    for c in range(NCH):
                        own_wait(dve, n)
                        nc.vector.bn_aggr(mv[:, 0, c, :], stat[:, 0, c, :]).then_inc(sem["dv_ln1"], 1)
                    dve.wait_ge(sem["dv_ln1"], at("dv_ln1", n, 2 * NCH))
                    nc.vector.tensor_scalar(rs[:, 0, :], mv[:, 0, :, 1], EPS, None, ALU.add)\
                        .then_inc(sem["dv_ln1"], 1)

                def normed_x(c):
                    dve.wait_ge(sem["po_p1"], at("po_p1", n, 1))
                    if C:
                        dve.wait_ge(sem["pe_x3t"], at("pe_x3t", p, KT))
                    nc.vector.tensor_scalar(xh[:, c, :], xb[1 - j][:, c, :], mv[:, 0, c, 0:1], rs[:, 0, c:c + 1],
                                            ALU.subtract, ALU.mult).then_inc(sem["dv_xh"], 1)

                def normed_y(c):
                    dve.wait_ge(sem["po_p4"], at("po_p4", p, c + 1))
                    nc.vector.tensor_scalar(y[:, c, :], y[:, c, :], mv[:, 3, c, 0:1], rs[:, 3, c:c + 1],
                                            ALU.subtract, ALU.mult).then_inc(sem["dv_t4"], 1)

                def ln4(c):
                    if c == 0:
                        dve.wait_ge(sem["b_in"], at("b_in", e, 32))
                    dve.wait_ge(sem["pe_f2"], at("pe_f2", p, c + 1))
                    nc.vector.tensor_tensor(y[:, c, :], PB[c % 2][:, 0:D], b2s[:, :], ALU.add)\
                        .then_inc(sem["dv_y4"], 1)
                    dve.wait_ge(sem["dv_y4"], at("dv_y4", p, c + 1))
                    stats_eps(3, y[:, c, :], c, "dv_ln4", p)

                def ln2(c):
                    dve.wait_ge(sem["ac_y"], at("ac_y", s, c + 1))
                    stats_eps(1, y[:, c, :], c, "dv_ln2", s)

                def mid(c):
                    dve.wait_ge(sem["po_p2"], at("po_p2", s, c + 1))
                    nc.vector.tensor_scalar(y[:, c, :], y[:, c, :], mv[:, 1, c, 0:1], rs[:, 1, c:c + 1],
                                            ALU.subtract, ALU.mult).then_inc(sem["dv_t"], 1)
                    dve.wait_ge(sem["dv_t"], at("dv_t", s, c + 1))
                    if C:
                        dve.wait_ge(sem["po_fin"], at("po_fin", p, NCH))
                    nc.vector.tensor_tensor(x2[:, c, :], y[:, c, :], xb[j][:, c, :], ALU.add)\
                        .then_inc(sem["dv_x2"], 1)
                    dve.wait_ge(sem["dv_x2"], at("dv_x2", s, c + 1))
                    stats_eps(2, x2[:, c, :], c, "dv_ln3", s)

                def ln3(c, b):
                    dve.wait_ge(sem["po_p3"], at("po_p3", b, c + 1))
                    nc.vector.tensor_scalar(xh[:, c, :], x2[:, c, :], mv[:, 2, c, 0:1], rs[:, 2, c:c + 1],
                                            ALU.subtract, ALU.mult).then_inc(sem["dv_xh3"], 1)

                def gates(tl):
                    dve.wait_ge(sem["ac_abs"], at("ac_abs", n, tl + 1))
                    nc.vector.tensor_scalar(gm[:, tl, :], PB[tl][:, :], gkb[:, tl:tl + 1], 0.0,
                                            ALU.add, ALU.min).then_inc(sem["dv_gl"], 1)

                def gate_sub():
                    dve.wait_ge(sem["ac_l"], at("ac_l", n, 1))
                    dve.wait_ge(sem["dv_gl"], at("dv_gl", n, KT))
                    nc.vector.tensor_tensor(gm[:, :, :], gm[:, :, :], gn[:, :, :], ALU.subtract)\
                        .then_inc(sem["dv_gsub"], 1)

                def q_evac(tl):
                    dve.wait_ge(sem["pe_q"], at("pe_q", n, tl + 1))
                    if B:
                        dve.wait_ge(sem["pe_att"], at("pe_att", s, NCH))
                    dve.wait_ge(sem["ac_k"], at("ac_k", n, tl + 1))
                    nc.vector.tensor_tensor(qk[:, tl, :], PB[tl][:, :], kk[:, tl, :], ALU.mult)\
                        .then_inc(sem["dv_q"], 1)
                    dve.wait_ge(sem["ac_a"], at("ac_a", n, 1))
                    for hh in range(2):
                        r = slice(hh * HK, (hh + 1) * HK)
                        nc.vector.scalar_tensor_tensor(qbd[r, tl, hh, :], PB[tl][r, :], QSCALE, ga[r, tl, :],
                                                       ALU.mult, ALU.mult).then_inc(sem["dv_q"], 1)

                if C:
                    ln3(3, p)
                if B:
                    dve.wait_ge(sem["pe_diag"], at("pe_diag", s, 1))
                    nc.vector.tensor_copy(dg[:, :], PO[:, 0:NCH * H]).then_inc(sem["dv_dg"], 1)
                for step in range(2 * NL):
                    if B:
                        if step // 2 < MASKED:
                            copy_pairs(step // 2, step % 2)
                        q_update(step // 2, step % 2)
                    if C:
                        if step == 1:
                            for kt in range(KT):
                                lo_part(xT_lo[:, kt, :], xT_hi[:, kt, :], PT[kt][:, :], "ac_x3hi", p, kt + 1, "dv_x3lo")
                        if 3 <= step < 3 + FT:
                            h_lo_part(step - 3)
                        if 12 <= step < 14:
                            ln4(step - 12)
                    if A:
                        if step == 10:
                            ln1_stats()
                        if step == 11:
                            ln1_aggregate()
                        if step == 12:
                            for c in range(NCH):
                                normed_x(c)
                if A:
                    for kt in range(KT):
                        lo_part(xT_lo[:, kt, :], xT_hi[:, kt, :], PT[kt][:, :], "ac_xhi", n, kt + 1, "dv_xlo")
                if C:
                    normed_y(0)
                    ln4(2)
                    normed_y(1)
                    ln4(3)
                    normed_y(2)
                if A:
                    gates(0)
                if C:
                    normed_y(3)
                if A:
                    gates(1)
                if B:
                    o_part(0)
                    state(0)
                    og(0)
                    o_part(1)
                    state(1)
                if A:
                    gate_sub()
                if B:
                    og(1)
                    state(2)
                    og_lo(0)
                    o_part(2)
                    ln2(0)
                    og(2)
                    og_lo(1)
                    o_part(3)
                if A:
                    q_evac(0)
                if B:
                    mid(0)
                    og_lo(2)
                    ln2(1)
                if A:
                    q_evac(1)
                if B:
                    og(3)
                    mid(1)
                    ln2(2)
                    og_lo(3)
                    ln3(0, s)
                    mid(2)
                    ln3(1, s)
                    ln2(3)
                    ln3(2, s)
                    mid(3)

            program(dve, run)

        @block.scalar
        def _(act):
            def run(s, j, e, B, C, A):
                p, n = s - 1, s + 1

                def copy(dst, src, name):
                    nc.scalar.activation(dst, src, ACT.Copy).then_inc(sem[name], 1)

                def gelu(m):
                    act.wait_ge(sem["pe_f1"], at("pe_f1", p, m + 1))
                    if m >= 2:
                        act.wait_ge(sem["dv_hlo"], at("dv_hlo", p, m - 1))
                    nc.scalar.activation(hf[:, m % 2, :], PB[m % 2][:, :], ACT.Gelu_apprx_tanh,
                                         bias=b1s[:, m:m + 1]).then_inc(sem["ac_gelu"], 1)
                    act.wait_ge(sem["ac_gelu"], at("ac_gelu", p, m + 1))
                    copy(h_hi[:, m, :], hf[:, m % 2, :], "ac_hhi")

                def weight_hi(c, en):
                    W, cols = ((W1, DF), (W2, D))[c]
                    act.wait_ge(sem["w_in"], at("w_in", en, 16 * (c + 1)))
                    if C:
                        act.wait_ge(sem[("pe_f1", "pe_f2")[c]], at(("pe_f1", "pe_f2")[c], p, (FT, NCH)[c]))
                    copy(W[0][:, :, :], raw[:, :].rearrange("p (k n) -> p k n", n=cols), "ac_ws")

                def copy_blocks(i, tl):
                    h = LV[i]
                    act.wait_ge(sem["pe_lv"], at("pe_lv", s, 2 * i + tl + 1))
                    for b in range(HC // h):
                        r = slice(2 * h * b, 2 * h * b + h)
                        copy(Am[r, tl, :, 2 * h * b + h:2 * h * (b + 1)],
                             PL[tl][r, :].rearrange("p (a n h) -> p a n h", a=2 * NCH, h=h)[:, :, b, :], "ac_cp")

                def squares(c):
                    act.wait_ge(sem["dv_o"], at("dv_o", s, H * (c + 1)))
                    if c:
                        act.wait_ge(sem["ac_sq"], at("ac_sq", s, H * c))
                    for hd in range(H):
                        nc.scalar.activation(junk[:, hd * HV:(hd + 1) * HV], o[:, c % 2, hd * HV:(hd + 1) * HV], ACT.Square,
                                             accum_out=ssq[:, c * H + hd:c * H + hd + 1]).then_inc(sem["ac_sq"], 1)

                def v_evac(c):
                    act.wait_ge(sem["pe_v"], at("pe_v", n, c + 1))
                    if B:
                        act.wait_ge(sem["dv_o"], at("dv_o", s, H * (c + 1)))
                    copy(v[:, c, :], PB[0][:, :], "ac_v")

                def g_evac(c):
                    act.wait_ge(sem["pe_g"], at("pe_g", n, c + 1))
                    if B:
                        act.wait_ge(sem["dv_og"], at("dv_og", s, H * (c + 1)))
                    nc.scalar.activation(gs[:, c, :], PB[1][:, :], ACT.Silu).then_inc(sem["ac_g"], 1)

                def og_hi(c):
                    act.wait_ge(sem["pe_ogt"], at("pe_ogt", s, c + 1))
                    if c:
                        act.wait_ge(sem["pe_wo"], at("pe_wo", s, c))
                    copy(ogT_hi[:, :, :], PT[c % 2][:, :].rearrange("p (k t) -> p k t", k=VT), "ac_oghi")

                def y_evac(c):
                    act.wait_ge(sem["pe_wo"], at("pe_wo", s, c + 1))
                    if c == 0 and C:
                        act.wait_ge(sem["st_out"], at("st_out", p, 16))
                    copy(y[:, c, :], PL[c % 2][:, 0:D], "ac_y")

                if C:
                    for kt in range(KT):
                        act.wait_ge(sem["pe_x3t"], at("pe_x3t", p, kt + 1))
                        copy(xT_hi[:, kt, :], PT[kt][:, :], "ac_x3hi")
                    act.wait_ge(sem["b_in"], at("b_in", e, 32))
                for step in range(1, 2 * NL):
                    if B and step // 2 >= MASKED:
                        copy_blocks(step // 2, step % 2)
                    if C and 2 <= step < 2 + FT:
                        gelu(step - 2)
                    if A and j == 0 and step == 11:
                        weight_hi(0, 0 if not C else e + 1)
                if A:
                    for kt in range(KT):
                        act.wait_ge(sem["pe_xt"], at("pe_xt", n, kt + 1))
                        copy(xT_hi[:, kt, :], PT[kt][:, :], "ac_xhi")
                if B:
                    for f in range(2):
                        act.wait_ge(sem["pe_kt"], at("pe_kt", s, f + 1))
                        copy(kT[:, 2 * f:2 * f + 2, :], PT[f][:, :].rearrange("p (c d) -> p c d", c=2), "ac_kt")
                if A:
                    for tl in range(KT):
                        act.wait_ge(sem["pe_gl"], at("pe_gl", n, tl + 1))
                        nc.scalar.activation(gn[:, tl, :], PB[tl][:, :], ACT.Abs, bias=gkb[:, tl:tl + 1])\
                            .then_inc(sem["ac_abs"], 1)
                    act.wait_ge(sem["ac_abs"], at("ac_abs", n, KT))
                    nc.scalar.activation(gn[:, :, :], gn[:, :, :], ACT.Exp, scale=-1.0).then_inc(sem["ac_e"], 1)
                if B:
                    squares(0)
                if A:
                    for tl in range(KT):
                        act.wait_ge(sem["pe_k"], at("pe_k", n, tl + 1))
                        copy(kk[:, tl, :], PB[tl][:, :], "ac_k")
                if B:
                    squares(1)
                if A:
                    act.wait_ge(sem["ac_e"], at("ac_e", n, 1))
                    nc.scalar.activation(gn[:, :, :], gn[:, :, :], ACT.Ln, bias=1.0).then_inc(sem["ac_l"], 1)
                    v_evac(0)
                    act.wait_ge(sem["dv_gsub"], at("dv_gsub", n, 1))
                    nc.scalar.activation(ga[:, :, :], gm[:, :, :], ACT.Exp, scale=1.0 / GATE_NORM)\
                        .then_inc(sem["ac_a"], 1)
                if B:
                    og_hi(0)
                if A:
                    g_evac(0)
                    v_evac(1)
                if B:
                    squares(2)
                    y_evac(0)
                    og_hi(1)
                if A:
                    g_evac(1)
                if B:
                    squares(3)
                    y_evac(1)
                    og_hi(2)
                if A:
                    v_evac(2)
                if B:
                    og_hi(3)
                    y_evac(2)
                if A:
                    g_evac(2)
                if B:
                    y_evac(3)
                if A:
                    v_evac(3)
                    g_evac(3)
                if A and j == 0:
                    weight_hi(1, 0 if not C else e + 1)

            program(act, run)

        @block.gpsimd
        def _(pool):
            nc.gpsimd.memset(ident[:, :], 1.0).then_inc(c_step, 1)
            nc.gpsimd.memset(masks[:, :, :], 1.0).then_inc(c_step, 1)
            nc.gpsimd.memset(ind[:, :], QSCALE).then_inc(c_step, 1)
            nc.gpsimd.memset(mhalf[:, :], -0.5).then_inc(c_step, 1)
            count = [4]

            def select(out, pattern, base, mult):
                pool.wait_ge(c_step, count[0])
                nc.gpsimd.affine_select(out=out, in_=out, compare_op=ALU.is_ge, fill=0.0, base=base,
                                        pattern=pattern, channel_multiplier=mult).then_inc(c_step, 1)
                count[0] += 1

            select(ident[:, :], [[1, P]], 0, -1)
            select(ident[:, :], [[-1, P]], 0, 1)
            select(ind[:, 0:1], [[0, 1]], HK - 1, -1)
            select(ind[:, 1:2], [[0, 1]], -HK, 1)
            for i in range(MASKED):
                h = LV[i]
                m = masks[:, i, :].rearrange("p (n h) -> p n h", h=h)
                select(m, [[-2 * h, HC // h], [0, h]], 0, 1)
                select(m, [[2 * h, HC // h], [0, h]], h - 1, -1)
            pool.wait_ge(c_step, count[0])
            nc.gpsimd.memset(ssq[:, :], 0.0).then_inc(c_ready, 1)
            pool.wait_ge(c_in, 64)

            def run(s, j, e, B, C, A):
                p, n = s - 1, s + 1

                def output(c):
                    pool.wait_ge(sem["dv_t4"], at("dv_t4", p, c + 1))
                    nc.gpsimd.tensor_tensor(y[:, c, :], y[:, c, :], x2[:, c, :], ALU.add)\
                        .then_inc(sem["po_fin"], 1)

                def block_totals(levels):
                    for i in levels:
                        if i:
                            pool.wait_ge(sem["po_tot"], at("po_tot", n, i))
                        else:
                            pool.wait_ge(sem["ac_a"], at("ac_a", n, 1))
                            if B:
                                pool.wait_ge(sem["dv_st"], at("dv_st", s, 4 * (NCH - 1)))
                                pool.wait_ge(sem["dv_qu"], at("dv_qu", s, 4 * NL))
                        t = totals(LV[i]).rearrange("p k (n t) -> p k n t", t=2)
                        nc.gpsimd.tensor_tensor(totals(2 * LV[i]), t[:, :, :, 0], t[:, :, :, 1], ALU.mult)\
                            .then_inc(sem["po_tot"], 1)

                def k_update(i, tl):
                    h = LV[i]
                    pool.wait_ge(sem["pe_lv"], at("pe_lv", s, 2 * i + tl + 1))
                    if i + tl == 0:
                        pool.wait_ge(sem["po_tot"], at("po_tot", s, NL))
                    k = halves(kk[:, tl, :], h)[:, :, 0, :]
                    t = totals(h)[:, tl, :].rearrange("p (n t a) -> p n t a", t=2, a=1)[:, :, 1, :]
                    nc.gpsimd.tensor_tensor(k, k, t.to_broadcast([P, T // (2 * h), h]), ALU.mult)\
                        .then_inc(sem["po_ku"], 1)

                def rsqrt(k, c, ready, b, name):
                    pool.wait_ge(sem[ready], at(ready, b, 3 * (c + 1)))
                    nc.gpsimd.tensor_tensor(rs[:, k, c:c + 1], rs[:, k, c:c + 1], mhalf[:, 0:1], ALU.pow)\
                        .then_inc(sem[name], 1)

                def o_rstd(c):
                    w = slice(c * H, (c + 1) * H)
                    pool.wait_ge(sem["ac_sq"], at("ac_sq", s, H * (c + 1)))
                    own_wait(pool, s)
                    nc.gpsimd.tensor_scalar(rso[:, w], ssq[:, w], 1.0 / HV, EPS, ALU.mult, ALU.add)\
                        .then_inc(sem["po_ro"], 1)
                    pool.wait_ge(sem["po_ro"], at("po_ro", s, 2 * c + 1))
                    nc.gpsimd.tensor_tensor(rso[:, w], rso[:, w], mhalf[:, w], ALU.pow)\
                        .then_inc(sem["po_ro"], 1)

                def gate_weight(c):
                    pool.wait_ge(sem["ac_g"], at("ac_g", s, c + 1))
                    nc.gpsimd.tensor_tensor(gs[:, c, :], gs[:, c, :], rmsb[:, :], ALU.mult)\
                        .then_inc(sem["po_gw"], 1)

                def weight_lo(c, part, en):
                    W, name = ((W1, "po_w1"), (W2, "po_w2"))[c]
                    w = RAW // 4
                    flat = [x[:, :, :].rearrange("p k n -> p (k n)")[:, part * w:(part + 1) * w] for x in W]
                    pool.wait_ge(sem["ac_ws"], at("ac_ws", en, c + 1))
                    nc.gpsimd.tensor_tensor(flat[1], raw[:, part * w:(part + 1) * w], flat[0].bitcast(F32),
                                            ALU.subtract).then_inc(sem[name], 1)

                split_w1 = A and j == 0
                next_e = 0 if not C else e + 1
                for step in range(2 * NL):
                    if B:
                        k_update(step // 2, step % 2)
                        if 5 <= step < 5 + NCH:
                            gate_weight(step - 5)
                    if C and j == 1 and 1 <= step < 5:
                        weight_lo(1, step - 1, e)
                    if A and step == 12:
                        pool.wait_ge(sem["dv_ln1"], at("dv_ln1", n, 2 * NCH + 1))
                        nc.gpsimd.tensor_tensor(rs[:, 0, :], rs[:, 0, :], mhalf[:, 0:NCH], ALU.pow)\
                            .then_inc(sem["po_p1"], 1)
                if C:
                    for c in range(NCH):
                        rsqrt(3, c, "dv_ln4", p, "po_p4")
                        if c:
                            output(c - 1)
                    output(3)
                if split_w1:
                    weight_lo(0, 0, next_e)
                    weight_lo(0, 1, next_e)
                if B:
                    o_rstd(0)
                if split_w1:
                    weight_lo(0, 2, next_e)
                if B:
                    o_rstd(1)
                if split_w1:
                    weight_lo(0, 3, next_e)
                if A:
                    block_totals([0, 1])
                if B:
                    rsqrt(1, 0, "dv_ln2", s, "po_p2")
                    o_rstd(2)
                if A:
                    block_totals([2, 3, 4, 5, 6])
                if B:
                    rsqrt(2, 0, "dv_ln3", s, "po_p3")
                    o_rstd(3)
                    rsqrt(1, 1, "dv_ln2", s, "po_p2")
                    rsqrt(2, 1, "dv_ln3", s, "po_p3")
                    rsqrt(1, 2, "dv_ln2", s, "po_p2")
                    rsqrt(2, 2, "dv_ln3", s, "po_p3")
                    rsqrt(1, 3, "dv_ln2", s, "po_p2")
                    rsqrt(2, 3, "dv_ln3", s, "po_p3")

            program(pool, run)


_IN = ["L0_attn_x", "L0_attn_Wq", "L0_attn_Wk", "L0_attn_Wv", "L0_attn_Wg", "L0_attn_gk_w1", "L0_attn_gk_w2",
       "L0_attn_gk_b", "L0_attn_Wo", "L0_attn_rms_w", "L0_ffn_w1", "L0_ffn_b1", "L0_ffn_w2", "L0_ffn_b2"]


def kernel(**inputs):
    import numpy as np
    import concourse.bacc as bacc
    from concourse import mybir
    from concourse.bass_utils import run_bass_kernel_spmd

    a = {n: np.asarray(inputs[n]) for n in _IN}
    P, H = 128, 4
    a["L0_attn_gk_w1"] = a["L0_attn_gk_w1"].T
    a["L0_attn_gk_b"] = a["L0_attn_gk_b"].reshape(-1, P).T
    a["L0_attn_rms_w"] = np.tile(a["L0_attn_rms_w"], (P, H))
    E = a["L0_ffn_b1"].shape[0]
    a["L0_ffn_b1"] = a["L0_ffn_b1"].reshape(E, -1, P).transpose(0, 2, 1)
    a["L0_ffn_b2"] = np.repeat(a["L0_ffn_b2"][:, None, :], P, axis=1)

    nc = bacc.Bacc("TRN2", target_bir_lowering=False, num_devices=1)
    arrays, args = {}, []
    for n in _IN:
        arrays[n] = np.ascontiguousarray(a[n])
        args.append(nc.dram_tensor(n, arrays[n].shape, mybir.dt.from_np(arrays[n].dtype), kind="ExternalInput").ap())
    shape = arrays["L0_attn_x"].shape
    args.append(nc.dram_tensor("out", shape, mybir.dt.float32, kind="ExternalOutput").ap())
    build(nc, *args)
    r = run_bass_kernel_spmd(nc, [arrays], core_ids=[0])
    return r.results[0]["out"]
```

```python
def build(nc, x_d, wq_d, wk_d, wv_d, wg_d, w1t_d, w2g_d, gkb_d, wo_d, rms_d,
          fw1_d, fb1_d, fw2_d, fb2_d, out_d):
    from contextlib import ExitStack
    from concourse import mybir

    F32, F32R, U32 = mybir.dt.float32, mybir.dt.float32r, mybir.dt.uint32
    ACT, ALU = mybir.ActivationFunctionType, mybir.AluOpType
    P = 128
    NB, T, D = x_d.shape
    E, _, DF = fw1_d.shape
    LR = w2g_d.shape[0]
    DV = wv_d.shape[1]
    H = 4
    HV = DV // H
    HK = D // H
    CH = 128
    NCH = T // CH
    KT = D // P
    FT = DF // P
    VT = DV // P
    LV = [1, 2, 4, 8, 16, 32, 64]
    NL = len(LV)
    MASKED = 5
    HC = CH // 2
    EPS = 1e-5
    QSCALE = HK ** -0.5
    GATE_NORM = 16.0
    SLOTS = NB

    ctx = ExitStack()
    with ctx:
        def sb(name, shape, dt=F32):
            return ctx.enter_context(nc.sbuf_tensor(name, shape, dt))

        def ps(name):
            return ctx.enter_context(nc.psum_tensor(name, [P, 512], F32))

        xb = [sb(f"x_in{j}", [P, NCH, D]) for j in range(2)]
        xh = sb("x_normed", [P, NCH, D])
        xT_hi, xT_lo = sb("xT_hi", [P, KT, T], F32R), sb("xT_lo", [P, KT, T], F32R)
        x2 = sb("x_mid", [P, NCH, D])
        y = sb("y", [P, NCH, D])
        qbd = sb("q_blockdiag", [P, KT, 2, T])
        kk = sb("k_decayed", [P, KT, T])
        ga = sb("gates", [P, KT, T])
        qk = sb("q_times_k", [P, KT, T])
        gn = qk
        tot = sb("block_totals", [P, KT, T])
        Am = sb("attn_T", [P, KT, NCH * 2, CH])
        kT = sb("k_tokens", [P, NCH, D])
        S = sb("state", [P, KT, HV])
        v = sb("v", [P, NCH, DV])
        gs = sb("out_gate", [P, NCH, DV])
        o = sb("o", [P, 2, DV])
        ogT_hi, ogT_lo = sb("ogT_hi", [P, VT, CH], F32R), sb("ogT_lo", [P, VT, CH], F32R)
        hf = sb("gelu_out", [P, 2, T])
        gm = qg = hf
        h_hi, h_lo = sb("h_hi", [P, FT, T], F32R), sb("h_lo", [P, FT, T], F32R)
        NA = 3 * D
        WA = [sb(f"w_qkg_{n}", [P, KT, NA], F32R) for n in ("hi", "lo")]
        WB = [sb(f"w_vg_{n}", [P, KT, 2 * DV], F32R) for n in ("hi", "lo")]
        WO = [sb(f"w_o_{n}", [P, VT, D], F32R) for n in ("hi", "lo")]
        W1 = [sb(f"w_ff1_{n}", [P, KT, DF], F32R) for n in ("hi", "lo")]
        W2 = [sb(f"w_ff2_{n}", [P, FT, D], F32R) for n in ("hi", "lo")]
        RAW = KT * DF
        raw = sb("w_raw", [P, RAW])
        masks = sb("level_masks", [P, MASKED, HC])
        rmsb = sb("rms_w_rows", [P, DV])
        b2s = sb("ff_b2_rows", [P, D])
        b1s = sb("ff_b1_cols", [P, FT])
        gkb = sb("gk_b_cols", [P, KT])
        ident = sb("ident", [P, P])
        ind = sb("head_sum", [P, 2])
        mhalf = sb("minus_half", [P, NCH * H])
        stat = sb("bn", [P, 4, NCH, 6])
        mv = sb("mean_var", [P, 4, NCH, 2])
        rs = sb("rstd", [P, 4, NCH])
        ssq = sb("o_sumsq", [P, NCH * H])
        rso = sb("o_rstd", [P, NCH * H])
        dg = sb("qk_diag", [P, NCH * H])
        junk = sb("square_out", [P, DV], mybir.dt.bfloat16)

        PB = [ps(f"ps_big{j}") for j in range(2)]
        PT = [ps(f"ps_transpose{j}") for j in range(2)]
        PL = [ps(f"ps_level{j}") for j in range(2)]
        PO, PS = ps("ps_out"), ps("ps_state")

        w1t, w2g = kT[0:LR, 0, :], kT[0:LR, 1, :]
        STAGED = [PB[0][:, :].rearrange("p (k n) -> p k n", k=KT),
                  x2[:, :, :].rearrange("p c d -> p (c d)").rearrange("p (k n) -> p k n", k=KT),
                  raw[:, :].rearrange("p (k n) -> p k n", k=KT),
                  y[:, :, :]]
        CONST_W = [[WA[i][:, :, 2 * D:], WA[i][:, :, 0:2 * D], WB[i][:, :, :], WO[i][:, :, :]] for i in range(2)]

        toff, used = {}, 0
        for h in LV[1:] + [CH]:
            toff[h] = used
            used += T // h

        def totals(h):
            return ga[:, :, :] if h == 1 else tot[:, :, toff[h]:toff[h] + T // h]

        PER = dict(
            x_in=16, st_out=16, w_in=32, b_in=32,
            pe_xt=KT, pe_gl=KT, pe_k=KT, pe_q=KT, pe_v=NCH, pe_g=NCH,
            pe_diag=1, pe_lv=2 * NL, pe_kt=2, pe_st=NCH - 1, pe_att=NCH, pe_ogt=NCH, pe_wo=NCH,
            pe_x3t=KT, pe_f1=FT, pe_f2=NCH,
            dv_ln1=2 * NCH + 1, dv_xh=NCH, dv_xlo=KT, dv_gl=KT, dv_gsub=1, dv_q=2 * KT,
            dv_dg=1, dv_cp=2 * MASKED, dv_qu=4 * NL, dv_st=4 * (NCH - 1), dv_o=NCH * H, dv_og=NCH * H,
            dv_oglo=NCH, dv_ln2=3 * NCH, dv_t=NCH, dv_ln3=3 * NCH,
            dv_xh3=NCH, dv_x3lo=KT, dv_hlo=FT, dv_y4=NCH, dv_ln4=3 * NCH, dv_t4=NCH,
            ac_xhi=KT, ac_abs=KT, ac_e=1, ac_l=1, ac_a=1, ac_k=KT, ac_v=NCH, ac_g=NCH, ac_qb=2 * KT,
            ac_cp=6, ac_kt=2, ac_sq=NCH * H, ac_oghi=NCH,
            ac_x3hi=KT, ac_gelu=FT, ac_hhi=FT, ac_ws=2,
            po_p1=1, po_p2=NCH, po_p3=NCH, po_p4=NCH, po_x2=NCH, po_fin=NCH, po_tot=NL, po_ku=2 * NL,
            po_gw=NCH, po_ro=2 * NCH, po_w1=4, po_w2=4,
        )
        sem = {n: ctx.enter_context(nc.semaphore(n)) for n in PER}
        c_bias = ctx.enter_context(nc.semaphore("const_bias_in"))
        c_w = [ctx.enter_context(nc.semaphore(f"const_{n}_in")) for n in ("gate", "qk", "vg", "o")]
        c_ready = ctx.enter_context(nc.semaphore("const_ready"))
        c_step = ctx.enter_context(nc.semaphore("const_step"))
        c_hi = ctx.enter_context(nc.semaphore("const_hi"))
        c_lo = ctx.enter_context(nc.semaphore("const_lo"))
        c_w12 = ctx.enter_context(nc.semaphore("const_w12"))

        def at(name, b, c):
            return b * PER[name] + c

        def own_wait(eng, b):
            if not isinstance(b, int):
                eng.nop(nofuse=True)

        def program(eng, run):
            run(-1, 1, 0, False, False, True)
            run(0, 0, 0, True, False, True)
            with eng.Fori(0, NB // 2 - 1) as i:
                run(i * 2 + 1, 1, i, True, True, True)
                run(i * 2 + 2, 0, i, True, True, True)
            run(NB - 1, 1, E - 1, True, True, False)
            run(NB, 0, E - 1, False, True, False)

        def halves(ap, h):
            return ap.rearrange("p (n t h) -> p n t h", t=2, h=h)

        block = ctx.enter_context(nc.Block())

        @block.sync
        def _(sp):
            sp.dma_start(w1t, w1t_d).then_inc(c_w[0], 16)
            sp.dma_start(w2g, w2g_d).then_inc(c_w[0], 16)
            sp.dma_start(gkb[:, :], gkb_d).then_inc(c_bias, 16)
            for k, srcs in ((1, [wq_d, wk_d]), (2, [wv_d, wg_d]), (3, [wo_d])):
                w = srcs[0].shape[1]
                for m, src in enumerate(srcs):
                    sp.dma_start(STAGED[k][:, :, m * w:(m + 1) * w],
                                 src.rearrange("(k p) n -> p k n", p=P)).then_inc(c_w[k], 16)
            sp.dma_start(rmsb[:, :], rms_d).then_inc(c_bias, 16)

            def load_w1(e, s, C):
                sp.dma_start(raw[:, :].rearrange("p (k n) -> p k n", k=KT),
                             fw1_d[e].rearrange("(k p) n -> p k n", p=P)).then_inc(sem["w_in"], 16)
                if C:
                    sp.wait_ge(sem["ac_gelu"], at("ac_gelu", s - 1, FT))
                    sp.wait_ge(sem["dv_y4"], at("dv_y4", s - 1, NCH))
                sp.dma_start(b1s[:, :], fb1_d[e]).then_inc(sem["b_in"], 16)
                sp.dma_start(b2s[:, :], fb2_d[e]).then_inc(sem["b_in"], 16)

            def load_w2(e):
                sp.wait_ge(sem["po_w1"], at("po_w1", e, 4))
                sp.dma_start(raw[:, :].rearrange("p (k n) -> p k n", k=FT),
                             fw2_d[e].rearrange("(k p) n -> p k n", p=P)).then_inc(sem["w_in"], 16)

            def run(s, j, e, B, C, A):
                if B and A:
                    if C:
                        sp.wait_ge(sem["po_x2"], at("po_x2", s - 1, NCH))
                    else:
                        sp.wait_ge(sem["dv_ln1"], at("dv_ln1", 0, NCH))
                    sp.dma_start(xb[1 - j][:, :, :],
                                 x_d[s + 1].rearrange("(c p) d -> p c d", p=P)).then_inc(sem["x_in"], 16)
                if B and A and j == 0:
                    if isinstance(s, int):
                        sp.wait_ge(c_lo, 4)
                        load_w1(0, s, C)
                    else:
                        sp.wait_ge(sem["po_w2"], at("po_w2", e, 4))
                        load_w1(e + 1, s, C)
                if C:
                    sp.wait_ge(sem["po_fin"], at("po_fin", s - 1, NCH))
                    sp.dma_start(out_d[s - 1].rearrange("(c p) d -> p c d", p=P),
                                 y[:, :, :]).then_inc(sem["st_out"], 16)
                if B and A and j == 0:
                    load_w2(0 if isinstance(s, int) else e + 1)

            program(sp, run)
            sp.wait_ge(sem["st_out"], 16 * NB)

        @block.tensor
        def _(pe):
            def three(out, lhs, rhs, first=True, final=True):
                n = len(lhs)
                for i in range(n):
                    (ah, al), (bh, bl) = lhs[i], rhs[i]
                    nc.tensor.matmul(out, ah, bh, start=(first and i == 0), stop=False)
                    nc.tensor.matmul(out, ah, bl, start=False, stop=False)
                    last = nc.tensor.matmul(out, al, bh, start=False, stop=(final and i == n - 1))
                return last

            pe.wait_ge(c_w[0], 32)
            for kt in range(KT):
                last = nc.tensor.matmul(PB[0][:, kt * D:(kt + 1) * D], w1t[:, kt * P:(kt + 1) * P],
                                        w2g, start=True, stop=True)
            last.then_inc(c_w12, 1)
            pe.wait_ge(c_ready, 1)

            def transpose_tokens(src, kt):
                for c in range(NCH):
                    last = nc.tensor.transpose(PT[kt][:, c * P:(c + 1) * P],
                                               src[:, c, kt * P:(kt + 1) * P], ident[:, :])
                return last

            def run(s, j, e, B, C, A):
                p, n = s - 1, s + 1

                def level(i, tl):
                    h = LV[i]
                    if i == 0:
                        if tl == 0:
                            pe.wait_ge(sem["ac_qb"], at("ac_qb", s, 2 * KT))
                            pe.wait_ge(sem["dv_q"], at("dv_q", s, 2 * KT))
                            if C:
                                pe.wait_ge(sem["dv_o"], at("dv_o", p, NCH * H))
                            pe.wait_ge(sem["ac_k"], at("ac_k", s, KT))
                        if C:
                            pe.wait_ge(sem["dv_t"], at("dv_t", p, 3 + tl))
                    else:
                        pe.wait_ge(sem["dv_qu"], at("dv_qu", s, 4 * (i - 1) + 2 * tl + 2))
                        pe.wait_ge(sem["po_ku"], at("po_ku", s, 2 * (i - 1) + tl + 1))
                        if i - 1 < MASKED:
                            pe.wait_ge(sem["dv_cp"], at("dv_cp", s, 2 * (i - 1) + tl + 1))
                        else:
                            pe.wait_ge(sem["ac_cp"], at("ac_cp", s, 2 * tl + 2))
                    for c in range(NCH):
                        q = qbd[:, tl, :, c * CH:(c + 1) * CH].rearrange("p a (n t h) -> p a n t h", t=2, h=h)
                        last = nc.tensor.matmul(PL[tl][:, c * CH:(c + 1) * CH],
                                                kk[:, tl, c * CH:(c + 1) * CH], q[:, :, :, 1, :],
                                                start=True, stop=True)
                        if i == 0:
                            self_product = diag(c, tl)
                    last.then_inc(sem["pe_lv"], 1)
                    if i + 1 == tl:
                        self_product.then_inc(sem["pe_diag"], 1)

                def diag(c, tl):
                    w = c * H + 2 * tl
                    return nc.tensor.matmul(PO[:, w:w + 2], qk[:, tl, c * CH:(c + 1) * CH], ind[:, :],
                                            start=True, stop=True)

                def x3t(kt):
                    pe.wait_ge(sem["dv_xh3"], at("dv_xh3", p, NCH))
                    pe.wait_ge(sem["dv_oglo"], at("dv_oglo", p, 3 + kt))
                    transpose_tokens(xh, kt).then_inc(sem["pe_x3t"], 1)

                def f1(m):
                    pe.wait_ge(sem["dv_x3lo"], at("dv_x3lo", p, KT))
                    pe.wait_ge(sem["po_w1"], at("po_w1", e, 4))
                    if m >= 2:
                        pe.wait_ge(sem["ac_gelu"], at("ac_gelu", p, m - 1))
                    elif B and m == 0:
                        pe.wait_ge(sem["ac_v"], at("ac_v", s, NCH))
                    elif B:
                        pe.wait_ge(sem["ac_g"], at("ac_g", s, NCH))
                    w = slice(m * P, (m + 1) * P)
                    three(PB[m % 2][:, :], [(W1[0][:, kt, w], W1[1][:, kt, w]) for kt in range(KT)],
                          [(xT_hi[:, kt, :], xT_lo[:, kt, :]) for kt in range(KT)]).then_inc(sem["pe_f1"], 1)

                def f2(c):
                    pe.wait_ge(sem["po_w2"], at("po_w2", e, 4))
                    if c >= 2:
                        pe.wait_ge(sem["dv_y4"], at("dv_y4", p, c - 1))
                    else:
                        pe.wait_ge(sem["ac_gelu"], at("ac_gelu", p, FT - 1 + c))
                    t = slice(c * CH, (c + 1) * CH)
                    for m in range(FT):
                        pe.wait_ge(sem["dv_hlo"], at("dv_hlo", p, m + 1))
                        last = three(PB[c % 2][:, 0:D], [(h_hi[:, m, t], h_lo[:, m, t])],
                                     [(W2[0][:, m, :], W2[1][:, m, :])], m == 0, m == FT - 1)
                    last.then_inc(sem["pe_f2"], 1)

                def kh(f):
                    pe.wait_ge(sem["po_ku"], at("po_ku", s, 2 * NL))
                    if A:
                        pe.wait_ge(sem["dv_xlo"], at("dv_xlo", n, f + 1))
                    elif C:
                        pe.wait_ge(sem["dv_x3lo"], at("dv_x3lo", p, f + 1))
                    for c in range(2):
                        for tl in range(KT):
                            w = (2 * f + c) * CH
                            last = nc.tensor.transpose(PT[f][:, c * D + tl * P:c * D + (tl + 1) * P],
                                                       kk[:, tl, w:w + CH], ident[:, :])
                    last.then_inc(sem["pe_kt"], 1)

                def xt(kt):
                    pe.wait_ge(sem["dv_xh"], at("dv_xh", n, NCH))
                    if C:
                        pe.wait_ge(sem["dv_x3lo"], at("dv_x3lo", p, kt + 1))
                    elif B:
                        pe.wait_ge(sem["dv_xlo"], at("dv_xlo", s, kt + 1))
                    transpose_tokens(xh, kt).then_inc(sem["pe_xt"], 1)

                def feature_tile(bank, col):
                    w = slice(col, col + P)
                    return three(bank[:, :], [(WA[0][:, kt, w], WA[1][:, kt, w]) for kt in range(KT)],
                                 [(xT_hi[:, kt, :], xT_lo[:, kt, :]) for kt in range(KT)])

                def token_tile(bank, c, half):
                    t, w = slice(c * CH, (c + 1) * CH), slice(half * DV, (half + 1) * DV)
                    return three(bank[:, :], [(xT_hi[:, kt, t], xT_lo[:, kt, t]) for kt in range(KT)],
                                 [(WB[0][:, kt, w], WB[1][:, kt, w]) for kt in range(KT)])

                def gl(tl):
                    if not B and not C:
                        pe.wait_ge(c_lo, 1)
                    pe.wait_ge(sem["dv_xlo"], at("dv_xlo", n, KT))
                    if C:
                        pe.wait_ge(sem["dv_y4"], at("dv_y4", p, 3 + tl))
                    elif B:
                        pe.wait_ge(sem[("ac_v", "ac_g")[tl]], at(("ac_v", "ac_g")[tl], s, NCH))
                    feature_tile(PB[tl], 2 * D + tl * P).then_inc(sem["pe_gl"], 1)

                def kp(tl):
                    if not B and not C:
                        pe.wait_ge(c_lo, 2)
                    pe.wait_ge(sem["dv_gl"], at("dv_gl", n, tl + 1))
                    feature_tile(PB[tl], D + tl * P).then_inc(sem["pe_k"], 1)

                def qp(tl):
                    pe.wait_ge(sem[("ac_v", "ac_g")[tl]], at(("ac_v", "ac_g")[tl], n, 2))
                    feature_tile(PB[tl], tl * P).then_inc(sem["pe_q"], 1)

                def vp(c):
                    if not B and not C:
                        pe.wait_ge(c_lo, 3)
                    if c == 0:
                        pe.wait_ge(sem["ac_k"], at("ac_k", n, 1))
                    elif c == 2:
                        pe.wait_ge(sem["dv_q"], at("dv_q", n, 2))
                    else:
                        pe.wait_ge(sem["ac_v"], at("ac_v", n, c))
                    token_tile(PB[0], c, 0).then_inc(sem["pe_v"], 1)

                def gp(c):
                    if c == 0:
                        pe.wait_ge(sem["ac_k"], at("ac_k", n, 2))
                    elif c == 2:
                        pe.wait_ge(sem["dv_q"], at("dv_q", n, 4))
                    else:
                        pe.wait_ge(sem["ac_g"], at("ac_g", n, c))
                    token_tile(PB[1], c, 1).then_inc(sem["pe_g"], 1)

                def st(c):
                    pe.wait_ge(sem["ac_kt"], at("ac_kt", s, c // 2 + 1))
                    pe.wait_ge(sem["ac_v"], at("ac_v", s, c + 1))
                    if c:
                        pe.wait_ge(sem["dv_st"], at("dv_st", s, 4 * c))
                    elif C:
                        pe.wait_ge(sem["dv_st"], at("dv_st", p, 4 * (NCH - 1)))
                    for tl in range(KT):
                        last = nc.tensor.matmul(PS[:, tl * 2 * HV:(tl + 1) * 2 * HV],
                                                kT[:, c, tl * P:(tl + 1) * P],
                                                v[:, c, tl * 2 * HV:(tl + 1) * 2 * HV], start=True, stop=True)
                    last.then_inc(sem["pe_st"], 1)

                def att(c):
                    pe.wait_ge(sem["dv_cp"], at("dv_cp", s, 2 * MASKED))
                    pe.wait_ge(sem["ac_cp"], at("ac_cp", s, 6))
                    pe.wait_ge(sem["dv_qu"], at("dv_qu", s, 4 * NL))
                    pe.wait_ge(sem["ac_v"], at("ac_v", s, c + 1))
                    if c:
                        pe.wait_ge(sem["dv_o"], at("dv_o", s, c * H))
                        pe.wait_ge(sem["dv_st"], at("dv_st", s, 4 * c))
                    else:
                        pe.wait_ge(sem["dv_dg"], at("dv_dg", s, 1))
                    for hd in range(H):
                        tl, hh = hd // 2, hd % 2
                        w = slice(hd * HV, (hd + 1) * HV)
                        last = nc.tensor.matmul(PO[:, w], Am[:, tl, 2 * c + hh, :], v[:, c, w],
                                                start=True, stop=(c == 0))
                        if c:
                            last = nc.tensor.matmul(PO[:, w], qbd[:, tl, hh, c * CH:(c + 1) * CH],
                                                    S[:, tl, :], start=False, stop=True)
                    last.then_inc(sem["pe_att"], 1)

                def ogt(c):
                    pe.wait_ge(sem["dv_og"], at("dv_og", s, H * (c + 1)))
                    if c >= 2:
                        pe.wait_ge(sem["dv_oglo"], at("dv_oglo", s, c - 1))
                    else:
                        pe.wait_ge(sem["ac_kt"], at("ac_kt", s, c + 1))
                    for k in range(VT):
                        last = nc.tensor.transpose(PT[c % 2][:, k * P:(k + 1) * P], o[:, c % 2, k * P:(k + 1) * P], ident[:, :])
                    last.then_inc(sem["pe_ogt"], 1)

                def wo(c):
                    if not C:
                        pe.wait_ge(c_lo, 4)
                    pe.wait_ge(sem["dv_oglo"], at("dv_oglo", s, c + 1))
                    if c >= 2:
                        pe.wait_ge(sem["dv_t"], at("dv_t", s, c - 1))
                    else:
                        pe.wait_ge(sem["ac_cp"], at("ac_cp", s, 5 + c))
                    three(PL[c % 2][:, 0:D], [(ogT_hi[:, k, :], ogT_lo[:, k, :]) for k in range(VT)],
                          [(WO[0][:, k, :], WO[1][:, k, :]) for k in range(VT)]).then_inc(sem["pe_wo"], 1)

                for step in range(2 * NL):
                    if B:
                        level(step // 2, step % 2)
                    if C:
                        if step == 1:
                            x3t(0)
                            x3t(1)
                        if 3 <= step < 3 + FT:
                            f1(step - 3)
                        if 11 <= step < 14:
                            f2(step - 11)
                if A:
                    xt(0)
                    xt(1)
                if C:
                    f2(3)
                if B:
                    kh(0)
                    kh(1)
                if A:
                    gl(0)
                    gl(1)
                if B:
                    st(0)
                    att(0)
                if A:
                    kp(0)
                    kp(1)
                if B:
                    st(1)
                    att(1)
                if A:
                    vp(0)
                if B:
                    ogt(0)
                if A:
                    gp(0)
                if B:
                    st(2)
                    att(2)
                    ogt(1)
                if A:
                    vp(1)
                if B:
                    wo(0)
                    att(3)
                if A:
                    gp(1)
                if B:
                    wo(1)
                    ogt(2)
                if A:
                    qp(0)
                if B:
                    wo(2)
                    ogt(3)
                if A:
                    qp(1)
                if B:
                    wo(3)
                if A:
                    vp(2)
                    gp(2)
                    vp(3)
                    gp(3)

            program(pe, run)

        @block.vector
        def _(dve):
            def const_lo(k):
                dve.wait_ge(c_hi, k + 1)
                nc.vector.tensor_tensor(CONST_W[1][k], STAGED[k], CONST_W[0][k].bitcast(F32),
                                        ALU.subtract).then_inc(c_lo, 1)

            def run(s, j, e, B, C, A):
                p, n = s - 1, s + 1

                def lo_part(lo, hi, bank, hi_done, b, c, name):
                    dve.wait_ge(sem[hi_done], at(hi_done, b, c))
                    nc.vector.tensor_tensor(lo, bank, hi.bitcast(F32), ALU.subtract).then_inc(sem[name], 1)

                def copy_pairs(i, tl):
                    h = LV[i]
                    dve.wait_ge(sem["pe_lv"], at("pe_lv", s, 2 * i + tl + 1))
                    dst = Am[:, tl, :, :].rearrange("p a (n t h) -> p a n t h", t=2, h=h)[:, :, :, 1, :]
                    src = PL[tl][:, :].rearrange("p (a n h) -> p a n h", a=2 * NCH, h=h)
                    m = masks[:, i, :].bitcast(U32).rearrange("p (a n h) -> p a n h", a=1, h=h)
                    own_wait(dve, s)
                    nc.vector.copy_predicated(dst, m.to_broadcast([P, 2 * NCH, HC // h, h]), src)\
                        .then_inc(sem["dv_cp"], 1)

                def q_update(i, tl):
                    h = LV[i]
                    dve.wait_ge(sem["pe_lv"], at("pe_lv", s, 2 * i + tl + 1))
                    dve.wait_ge(sem["po_tot"], at("po_tot", s, NL))
                    for hh in range(2):
                        r = slice(hh * HK, (hh + 1) * HK)
                        q = halves(qbd[r, tl, hh, :], h)[:, :, 1, :]
                        t = totals(h)[r, tl, :].rearrange("p (n t a) -> p n t a", t=2, a=1)[:, :, 0, :]
                        nc.vector.tensor_tensor(q, q, t.to_broadcast([HK, T // (2 * h), h]), ALU.mult)\
                            .then_inc(sem["dv_qu"], 1)

                def h_lo_part(m):
                    dve.wait_ge(sem["ac_hhi"], at("ac_hhi", p, m + 1))
                    nc.vector.tensor_tensor(h_lo[:, m, :], hf[:, m % 2, :], h_hi[:, m, :].bitcast(F32),
                                            ALU.subtract).then_inc(sem["dv_hlo"], 1)

                def o_part(c):
                    dve.wait_ge(sem["pe_att"], at("pe_att", s, c + 1))
                    if c >= 2:
                        dve.wait_ge(sem["pe_ogt"], at("pe_ogt", s, c - 1))
                    elif c == 0:
                        dve.wait_ge(sem["dv_dg"], at("dv_dg", s, 1))
                    for hd in range(H):
                        w = slice(hd * HV, (hd + 1) * HV)
                        nc.vector.scalar_tensor_tensor(o[:, c % 2, w], v[:, c, w], dg[:, c * H + hd:c * H + hd + 1],
                                                       PO[:, w], ALU.mult, ALU.add).then_inc(sem["dv_o"], 1)

                def state(c):
                    dve.wait_ge(sem["pe_st"], at("pe_st", s, c + 1))
                    dve.wait_ge(sem["pe_att"], at("pe_att", s, c + 1))
                    if c:
                        dve.wait_ge(sem["dv_st"], at("dv_st", s, 4 * c))
                    for tl in range(KT):
                        for hh in range(2):
                            r = slice(hh * HK, (hh + 1) * HK)
                            w = slice(tl * 2 * HV + hh * HV, tl * 2 * HV + (hh + 1) * HV)
                            if c == 0:
                                ins = nc.vector.tensor_copy(S[r, tl, :], PS[r, w])
                            else:
                                t = totals(CH)[r, tl, c:c + 1]
                                ins = nc.vector.scalar_tensor_tensor(S[r, tl, :], S[r, tl, :], t, PS[r, w],
                                                                     ALU.mult, ALU.add)
                            ins.then_inc(sem["dv_st"], 1)

                def og(c):
                    dve.wait_ge(sem["po_ro"], at("po_ro", s, 2 * (c + 1)))
                    dve.wait_ge(sem["po_gw"], at("po_gw", s, c + 1))
                    for hd in range(H):
                        w = slice(hd * HV, (hd + 1) * HV)
                        nc.vector.scalar_tensor_tensor(o[:, c % 2, w], o[:, c % 2, w], rso[:, c * H + hd:c * H + hd + 1],
                                                       gs[:, c, w], ALU.mult, ALU.mult).then_inc(sem["dv_og"], 1)

                def og_lo(c):
                    lo_part(ogT_lo[:, :, :], ogT_hi[:, :, :],
                            PT[c % 2][:, :].rearrange("p (k t) -> p k t", k=VT), "ac_oghi", s, c + 1, "dv_oglo")

                def stats_eps(k, src, c, name, b):
                    nc.vector.bn_stats(stat[:, k, c, :], src).then_inc(sem[name], 1)
                    dve.wait_ge(sem[name], at(name, b, 3 * c + 1))
                    own_wait(dve, b)
                    nc.vector.bn_aggr(mv[:, k, c, :], stat[:, k, c, :]).then_inc(sem[name], 1)
                    dve.wait_ge(sem[name], at(name, b, 3 * c + 2))
                    nc.vector.tensor_scalar(rs[:, k, c:c + 1], mv[:, k, c, 1:2], EPS, None, ALU.add)\
                        .then_inc(sem[name], 1)

                def ln1_stats():
                    dve.wait_ge(sem["x_in"], at("x_in", n, 16))
                    for c in range(NCH):
                        nc.vector.bn_stats(stat[:, 0, c, :], xb[1 - j][:, c, :]).then_inc(sem["dv_ln1"], 1)

                def ln1_aggregate():
                    dve.wait_ge(sem["dv_ln1"], at("dv_ln1", n, NCH))
                    for c in range(NCH):
                        own_wait(dve, n)
                        nc.vector.bn_aggr(mv[:, 0, c, :], stat[:, 0, c, :]).then_inc(sem["dv_ln1"], 1)
                    dve.wait_ge(sem["dv_ln1"], at("dv_ln1", n, 2 * NCH))
                    nc.vector.tensor_scalar(rs[:, 0, :], mv[:, 0, :, 1], EPS, None, ALU.add)\
                        .then_inc(sem["dv_ln1"], 1)

                def normed_x(c):
                    dve.wait_ge(sem["po_p1"], at("po_p1", n, 1))
                    if C:
                        dve.wait_ge(sem["pe_x3t"], at("pe_x3t", p, KT))
                    nc.vector.tensor_scalar(xh[:, c, :], xb[1 - j][:, c, :], mv[:, 0, c, 0:1], rs[:, 0, c:c + 1],
                                            ALU.subtract, ALU.mult).then_inc(sem["dv_xh"], 1)

                def normed_y(c):
                    dve.wait_ge(sem["po_p4"], at("po_p4", p, c + 1))
                    nc.vector.tensor_scalar(y[:, c, :], y[:, c, :], mv[:, 3, c, 0:1], rs[:, 3, c:c + 1],
                                            ALU.subtract, ALU.mult).then_inc(sem["dv_t4"], 1)

                def ln4(c):
                    if c == 0:
                        dve.wait_ge(sem["b_in"], at("b_in", e, 32))
                    dve.wait_ge(sem["pe_f2"], at("pe_f2", p, c + 1))
                    nc.vector.tensor_tensor(y[:, c, :], PB[c % 2][:, 0:D], b2s[:, :], ALU.add)\
                        .then_inc(sem["dv_y4"], 1)
                    dve.wait_ge(sem["dv_y4"], at("dv_y4", p, c + 1))
                    stats_eps(3, y[:, c, :], c, "dv_ln4", p)

                def ln2(c):
                    dve.wait_ge(sem["pe_wo"], at("pe_wo", s, c + 1))
                    stats_eps(1, PL[c % 2][:, 0:D], c, "dv_ln2", s)

                def normed_attn(c):
                    dve.wait_ge(sem["po_p2"], at("po_p2", s, c + 1))
                    if c == 0 and C:
                        dve.wait_ge(sem["st_out"], at("st_out", p, 16))
                    nc.vector.tensor_scalar(y[:, c, :], PL[c % 2][:, 0:D], mv[:, 1, c, 0:1], rs[:, 1, c:c + 1],
                                            ALU.subtract, ALU.mult).then_inc(sem["dv_t"], 1)

                def ln3_stats(c):
                    dve.wait_ge(sem["po_x2"], at("po_x2", s, c + 1))
                    stats_eps(2, x2[:, c, :], c, "dv_ln3", s)

                def ln3(c, b):
                    dve.wait_ge(sem["po_p3"], at("po_p3", b, c + 1))
                    nc.vector.tensor_scalar(xh[:, c, :], x2[:, c, :], mv[:, 2, c, 0:1], rs[:, 2, c:c + 1],
                                            ALU.subtract, ALU.mult).then_inc(sem["dv_xh3"], 1)

                def gates(tl):
                    dve.wait_ge(sem["ac_abs"], at("ac_abs", n, tl + 1))
                    nc.vector.tensor_scalar(gm[:, tl, :], PB[tl][:, :], gkb[:, tl:tl + 1], 0.0,
                                            ALU.add, ALU.min).then_inc(sem["dv_gl"], 1)

                def gate_sub():
                    dve.wait_ge(sem["ac_l"], at("ac_l", n, 1))
                    dve.wait_ge(sem["dv_gl"], at("dv_gl", n, KT))
                    nc.vector.tensor_tensor(gm[:, :, :], gm[:, :, :], gn[:, :, :], ALU.subtract)\
                        .then_inc(sem["dv_gsub"], 1)

                def q_evac(tl):
                    dve.wait_ge(sem["pe_q"], at("pe_q", n, tl + 1))
                    dve.wait_ge(sem["ac_k"], at("ac_k", n, tl + 1))
                    nc.vector.tensor_tensor(qk[:, tl, :], PB[tl][:, :], kk[:, tl, :], ALU.mult)\
                        .then_inc(sem["dv_q"], 1)
                    dve.wait_ge(sem["ac_a"], at("ac_a", n, 1))
                    nc.vector.scalar_tensor_tensor(qg[:, tl, :], PB[tl][:, :], QSCALE, ga[:, tl, :],
                                                   ALU.mult, ALU.mult).then_inc(sem["dv_q"], 1)

                if C:
                    ln3(3, p)
                for step in range(2 * NL):
                    if B and step == 1:
                        dve.wait_ge(sem["pe_diag"], at("pe_diag", s, 1))
                        nc.vector.tensor_copy(dg[:, :], PO[:, 0:NCH * H]).then_inc(sem["dv_dg"], 1)
                    if B:
                        if step // 2 < MASKED:
                            copy_pairs(step // 2, step % 2)
                        q_update(step // 2, step % 2)
                    if C:
                        if step == 1:
                            for kt in range(KT):
                                lo_part(xT_lo[:, kt, :], xT_hi[:, kt, :], PT[kt][:, :], "ac_x3hi", p, kt + 1, "dv_x3lo")
                        if 4 <= step < 4 + FT:
                            h_lo_part(step - 4)
                        if 12 <= step < 14:
                            ln4(step - 12)
                    if A:
                        if step == 10:
                            ln1_stats()
                        if step == 11:
                            ln1_aggregate()
                        if step == 12:
                            if not B and not C:
                                const_lo(0)
                            for c in range(NCH):
                                normed_x(c)
                            if not B and not C:
                                const_lo(1)
                if A:
                    for kt in range(KT):
                        lo_part(xT_lo[:, kt, :], xT_hi[:, kt, :], PT[kt][:, :], "ac_xhi", n, kt + 1, "dv_xlo")
                if C:
                    normed_y(0)
                    ln4(2)
                    normed_y(1)
                    ln4(3)
                    normed_y(2)
                if A:
                    if not B and not C:
                        dve.wait_ge(c_bias, 32)
                        const_lo(2)
                    gates(0)
                if C:
                    normed_y(3)
                if A:
                    gates(1)
                if B:
                    o_part(0)
                    state(0)
                    og(0)
                    o_part(1)
                    state(1)
                if A:
                    gate_sub()
                if B:
                    og_lo(0)
                    og(1)
                    state(2)
                    o_part(2)
                    ln2(0)
                    og_lo(1)
                    o_part(3)
                    og(2)
                    normed_attn(0)
                    ln2(1)
                    og_lo(2)
                    og(3)
                    normed_attn(1)
                if A:
                    q_evac(0)
                if B:
                    og_lo(3)
                if A:
                    q_evac(1)
                    if not B and not C:
                        dve.wait_ge(c_ready, 3)
                        const_lo(3)
                if B:
                    ln3_stats(0)
                    ln2(2)
                    ln2(3)
                    ln3(0, s)
                    ln3_stats(1)
                    normed_attn(2)
                    normed_attn(3)
                    ln3(1, s)
                    ln3_stats(2)
                    ln3_stats(3)
                    ln3(2, s)

            program(dve, run)

        @block.scalar
        def _(act):
            act.dma_start(xb[0][:, :, :], x_d[0].rearrange("(c p) d -> p c d", p=P)).then_inc(sem["x_in"], 16)

            def const_hi(k):
                if k:
                    act.wait_ge(c_w[k], 16 * (1 if k == 3 else 2))
                else:
                    act.wait_ge(c_w12, 1)
                nc.scalar.activation(CONST_W[0][k], STAGED[k], ACT.Copy).then_inc(c_hi, 1)

            const_hi(0)
            const_hi(1)

            def run(s, j, e, B, C, A):
                p, n = s - 1, s + 1

                def copy(dst, src, name):
                    nc.scalar.activation(dst, src, ACT.Copy).then_inc(sem[name], 1)

                def gelu(m):
                    act.wait_ge(sem["pe_f1"], at("pe_f1", p, m + 1))
                    if m >= 2:
                        act.wait_ge(sem["dv_hlo"], at("dv_hlo", p, m - 1))
                    nc.scalar.activation(hf[:, m % 2, :], PB[m % 2][:, :], ACT.Gelu_apprx_tanh,
                                         bias=b1s[:, m:m + 1]).then_inc(sem["ac_gelu"], 1)
                    act.wait_ge(sem["ac_gelu"], at("ac_gelu", p, m + 1))
                    copy(h_hi[:, m, :], hf[:, m % 2, :], "ac_hhi")

                def weight_hi(c, en):
                    W, cols = ((W1, DF), (W2, D))[c]
                    act.wait_ge(sem["w_in"], at("w_in", en, 16 * (c + 1)))
                    if C:
                        act.wait_ge(sem[("pe_f1", "pe_f2")[c]], at(("pe_f1", "pe_f2")[c], p, (FT, NCH)[c]))
                    copy(W[0][:, :, :], raw[:, :].rearrange("p (k n) -> p k n", n=cols), "ac_ws")

                def copy_blocks(i, tl):
                    h = LV[i]
                    act.wait_ge(sem["pe_lv"], at("pe_lv", s, 2 * i + tl + 1))
                    for b in range(HC // h):
                        r = slice(2 * h * b, 2 * h * b + h)
                        copy(Am[r, tl, :, 2 * h * b + h:2 * h * (b + 1)],
                             PL[tl][r, :].rearrange("p (a n h) -> p a n h", a=2 * NCH, h=h)[:, :, b, :], "ac_cp")

                def squares(c):
                    act.wait_ge(sem["dv_o"], at("dv_o", s, H * (c + 1)))
                    if c:
                        act.wait_ge(sem["ac_sq"], at("ac_sq", s, H * c))
                    for hd in range(H):
                        nc.scalar.activation(junk[:, hd * HV:(hd + 1) * HV], o[:, c % 2, hd * HV:(hd + 1) * HV], ACT.Square,
                                             accum_out=ssq[:, c * H + hd:c * H + hd + 1]).then_inc(sem["ac_sq"], 1)

                def v_evac(c):
                    act.wait_ge(sem["pe_v"], at("pe_v", n, c + 1))
                    if B:
                        act.wait_ge(sem["dv_o"], at("dv_o", s, H * (c + 1)))
                    copy(v[:, c, :], PB[0][:, :], "ac_v")

                def g_evac(c):
                    act.wait_ge(sem["pe_g"], at("pe_g", n, c + 1))
                    if B:
                        act.wait_ge(sem["dv_og"], at("dv_og", s, H * (c + 1)))
                    nc.scalar.activation(gs[:, c, :], PB[1][:, :], ACT.Silu).then_inc(sem["ac_g"], 1)

                def q_blocks(tl):
                    act.wait_ge(sem["dv_q"], at("dv_q", n, 2 * tl + 2))
                    if B:
                        act.wait_ge(sem["pe_att"], at("pe_att", s, NCH))
                    else:
                        act.wait_ge(c_ready, 3)
                    for hh in range(2):
                        r = slice(hh * HK, (hh + 1) * HK)
                        copy(qbd[r, tl, hh, :], qg[r, tl, :], "ac_qb")

                def og_hi(c):
                    act.wait_ge(sem["pe_ogt"], at("pe_ogt", s, c + 1))
                    if c:
                        act.wait_ge(sem["pe_wo"], at("pe_wo", s, c))
                    copy(ogT_hi[:, :, :], PT[c % 2][:, :].rearrange("p (k t) -> p k t", k=VT), "ac_oghi")

                if C:
                    for kt in range(KT):
                        act.wait_ge(sem["pe_x3t"], at("pe_x3t", p, kt + 1))
                        copy(xT_hi[:, kt, :], PT[kt][:, :], "ac_x3hi")
                    act.wait_ge(sem["b_in"], at("b_in", e, 32))
                for step in range(1, 2 * NL):
                    if B and step // 2 >= MASKED:
                        copy_blocks(step // 2, step % 2)
                    if C and 3 <= step < 3 + FT:
                        gelu(step - 3)
                    if A and j == 0 and step == 11:
                        weight_hi(0, 0 if not C else e + 1)
                if A:
                    for kt in range(KT):
                        act.wait_ge(sem["pe_xt"], at("pe_xt", n, kt + 1))
                        copy(xT_hi[:, kt, :], PT[kt][:, :], "ac_xhi")
                    if not B and not C:
                        act.wait_ge(c_bias, 32)
                        const_hi(2)
                if B:
                    for f in range(2):
                        act.wait_ge(sem["pe_kt"], at("pe_kt", s, f + 1))
                        copy(kT[:, 2 * f:2 * f + 2, :], PT[f][:, :].rearrange("p (c d) -> p c d", c=2), "ac_kt")
                if A:
                    for tl in range(KT):
                        act.wait_ge(sem["pe_gl"], at("pe_gl", n, tl + 1))
                        nc.scalar.activation(gn[:, tl, :], PB[tl][:, :], ACT.Abs, bias=gkb[:, tl:tl + 1])\
                            .then_inc(sem["ac_abs"], 1)
                    act.wait_ge(sem["ac_abs"], at("ac_abs", n, KT))
                    nc.scalar.activation(gn[:, :, :], gn[:, :, :], ACT.Exp, scale=-1.0).then_inc(sem["ac_e"], 1)
                if B:
                    squares(0)
                if A:
                    for tl in range(KT):
                        act.wait_ge(sem["pe_k"], at("pe_k", n, tl + 1))
                        copy(kk[:, tl, :], PB[tl][:, :], "ac_k")
                    if not B and not C:
                        v_evac(0)
                    act.wait_ge(sem["ac_e"], at("ac_e", n, 1))
                    nc.scalar.activation(gn[:, :, :], gn[:, :, :], ACT.Ln, bias=1.0).then_inc(sem["ac_l"], 1)
                if B:
                    squares(1)
                    og_hi(0)
                if A:
                    if B or C:
                        v_evac(0)
                    act.wait_ge(sem["dv_gsub"], at("dv_gsub", n, 1))
                    nc.scalar.activation(ga[:, :, :], gm[:, :, :], ACT.Exp, scale=1.0 / GATE_NORM)\
                        .then_inc(sem["ac_a"], 1)
                    g_evac(0)
                    v_evac(1)
                if B:
                    squares(2)
                    og_hi(1)
                    squares(3)
                if A:
                    g_evac(1)
                    if not B and not C:
                        const_hi(3)
                if B:
                    og_hi(2)
                    og_hi(3)
                if A:
                    q_blocks(0)
                    v_evac(2)
                    q_blocks(1)
                    g_evac(2)
                    v_evac(3)
                    g_evac(3)
                if A and j == 0:
                    weight_hi(1, 0 if not C else e + 1)

            program(act, run)

        @block.gpsimd
        def _(pool):
            count = [0]

            def fill(out, value):
                nc.gpsimd.memset(out, value).then_inc(c_step, 1)
                count[0] += 1

            def select(out, pattern, base, mult):
                pool.wait_ge(c_step, count[0])
                nc.gpsimd.affine_select(out=out, in_=out, compare_op=ALU.is_ge, fill=0.0, base=base,
                                        pattern=pattern, channel_multiplier=mult).then_inc(c_step, 1)
                count[0] += 1

            fill(mhalf[:, :], -0.5)
            fill(ident[:, :], 1.0)
            select(ident[:, :], [[1, P]], 0, -1)
            select(ident[:, :], [[-1, P]], 0, 1)
            pool.wait_ge(c_step, count[0])
            nc.gpsimd.memset(ssq[:, :], 0.0).then_inc(c_ready, 1)

            def late_constants():
                nc.gpsimd.memset(qbd[:, :, :, :], 0.0).then_inc(c_ready, 1)
                fill(masks[:, :, :], 1.0)
                fill(ind[:, :], QSCALE)
                select(ind[:, 0:1], [[0, 1]], HK - 1, -1)
                select(ind[:, 1:2], [[0, 1]], -HK, 1)
                for i in range(MASKED):
                    h = LV[i]
                    m = masks[:, i, :].rearrange("p (n h) -> p n h", h=h)
                    select(m, [[-2 * h, HC // h], [0, h]], 0, 1)
                    select(m, [[2 * h, HC // h], [0, h]], h - 1, -1)
                pool.wait_ge(c_step, count[0])
                nc.gpsimd.memset(Am[:, :, :, :], 0.0).then_inc(c_ready, 1)
                pool.wait_ge(c_bias, 32)

            def run(s, j, e, B, C, A):
                p, n = s - 1, s + 1

                def output(c):
                    pool.wait_ge(sem["dv_t4"], at("dv_t4", p, c + 1))
                    nc.gpsimd.tensor_tensor(y[:, c, :], y[:, c, :], x2[:, c, :], ALU.add)\
                        .then_inc(sem["po_fin"], 1)

                def block_totals(levels):
                    for i in levels:
                        if i:
                            pool.wait_ge(sem["po_tot"], at("po_tot", n, i))
                        else:
                            pool.wait_ge(sem["ac_a"], at("ac_a", n, 1))
                            if B:
                                pool.wait_ge(sem["dv_st"], at("dv_st", s, 4 * (NCH - 1)))
                                pool.wait_ge(sem["dv_qu"], at("dv_qu", s, 4 * NL))
                        t = totals(LV[i]).rearrange("p k (n t) -> p k n t", t=2)
                        nc.gpsimd.tensor_tensor(totals(2 * LV[i]), t[:, :, :, 0], t[:, :, :, 1], ALU.mult)\
                            .then_inc(sem["po_tot"], 1)

                def k_update(i, tl):
                    h = LV[i]
                    pool.wait_ge(sem["pe_lv"], at("pe_lv", s, 2 * i + tl + 1))
                    if i + tl == 0:
                        pool.wait_ge(sem["po_tot"], at("po_tot", s, NL))
                    k = halves(kk[:, tl, :], h)[:, :, 0, :]
                    t = totals(h)[:, tl, :].rearrange("p (n t a) -> p n t a", t=2, a=1)[:, :, 1, :]
                    nc.gpsimd.tensor_tensor(k, k, t.to_broadcast([P, T // (2 * h), h]), ALU.mult)\
                        .then_inc(sem["po_ku"], 1)

                def rsqrt(k, c, ready, b, name):
                    pool.wait_ge(sem[ready], at(ready, b, 3 * (c + 1)))
                    nc.gpsimd.tensor_tensor(rs[:, k, c:c + 1], rs[:, k, c:c + 1], mhalf[:, 0:1], ALU.pow)\
                        .then_inc(sem[name], 1)

                def residual(c):
                    pool.wait_ge(sem["dv_t"], at("dv_t", s, c + 1))
                    nc.gpsimd.tensor_tensor(x2[:, c, :], y[:, c, :], xb[j][:, c, :], ALU.add)\
                        .then_inc(sem["po_x2"], 1)

                def o_rstd(c):
                    w = slice(c * H, (c + 1) * H)
                    pool.wait_ge(sem["ac_sq"], at("ac_sq", s, H * (c + 1)))
                    own_wait(pool, s)
                    nc.gpsimd.tensor_scalar(rso[:, w], ssq[:, w], 1.0 / HV, EPS, ALU.mult, ALU.add)\
                        .then_inc(sem["po_ro"], 1)
                    pool.wait_ge(sem["po_ro"], at("po_ro", s, 2 * c + 1))
                    nc.gpsimd.tensor_tensor(rso[:, w], rso[:, w], mhalf[:, w], ALU.pow)\
                        .then_inc(sem["po_ro"], 1)

                def gate_weight(c):
                    pool.wait_ge(sem["ac_g"], at("ac_g", s, c + 1))
                    nc.gpsimd.tensor_tensor(gs[:, c, :], gs[:, c, :], rmsb[:, :], ALU.mult)\
                        .then_inc(sem["po_gw"], 1)

                def weight_lo(c, part, en):
                    W, name = ((W1, "po_w1"), (W2, "po_w2"))[c]
                    w = RAW // 4
                    flat = [x[:, :, :].rearrange("p k n -> p (k n)")[:, part * w:(part + 1) * w] for x in W]
                    pool.wait_ge(sem["ac_ws"], at("ac_ws", en, c + 1))
                    nc.gpsimd.tensor_tensor(flat[1], raw[:, part * w:(part + 1) * w], flat[0].bitcast(F32),
                                            ALU.subtract).then_inc(sem[name], 1)

                split_w1 = A and j == 0
                next_e = 0 if not C else e + 1
                for step in range(2 * NL):
                    if B:
                        k_update(step // 2, step % 2)
                        if 5 <= step < 5 + NCH:
                            gate_weight(step - 5)
                    if C and j == 1 and 1 <= step < 5:
                        weight_lo(1, step - 1, e)
                    if A and step == 12:
                        pool.wait_ge(sem["dv_ln1"], at("dv_ln1", n, 2 * NCH + 1))
                        nc.gpsimd.tensor_tensor(rs[:, 0, :], rs[:, 0, :], mhalf[:, 0:NCH], ALU.pow)\
                            .then_inc(sem["po_p1"], 1)
                        if not B and not C:
                            late_constants()
                if C:
                    for c in range(NCH):
                        rsqrt(3, c, "dv_ln4", p, "po_p4")
                        if c:
                            output(c - 1)
                    output(3)
                if split_w1:
                    weight_lo(0, 0, next_e)
                    weight_lo(0, 1, next_e)
                if B:
                    o_rstd(0)
                if split_w1:
                    weight_lo(0, 2, next_e)
                if B:
                    o_rstd(1)
                if split_w1:
                    weight_lo(0, 3, next_e)
                if A:
                    block_totals([0, 1])
                if B:
                    o_rstd(2)
                    rsqrt(1, 0, "dv_ln2", s, "po_p2")
                    o_rstd(3)
                    residual(0)
                    rsqrt(1, 1, "dv_ln2", s, "po_p2")
                if A:
                    block_totals([2, 3, 4])
                if B:
                    residual(1)
                    rsqrt(2, 0, "dv_ln3", s, "po_p3")
                if A:
                    block_totals([5, 6])
                if B:
                    rsqrt(1, 2, "dv_ln2", s, "po_p2")
                    rsqrt(1, 3, "dv_ln2", s, "po_p2")
                    rsqrt(2, 1, "dv_ln3", s, "po_p3")
                    residual(2)
                    residual(3)
                    rsqrt(2, 2, "dv_ln3", s, "po_p3")
                    rsqrt(2, 3, "dv_ln3", s, "po_p3")

            program(pool, run)


_IN = ["L0_attn_x", "L0_attn_Wq", "L0_attn_Wk", "L0_attn_Wv", "L0_attn_Wg", "L0_attn_gk_w1", "L0_attn_gk_w2",
       "L0_attn_gk_b", "L0_attn_Wo", "L0_attn_rms_w", "L0_ffn_w1", "L0_ffn_b1", "L0_ffn_w2", "L0_ffn_b2"]


def kernel(**inputs):
    import numpy as np
    import concourse.bacc as bacc
    from concourse import mybir
    from concourse.bass_utils import run_bass_kernel_spmd

    a = {n: np.asarray(inputs[n]) for n in _IN}
    P, H = 128, 4
    a["L0_attn_gk_w1"] = a["L0_attn_gk_w1"].T
    a["L0_attn_gk_b"] = a["L0_attn_gk_b"].reshape(-1, P).T
    a["L0_attn_rms_w"] = np.tile(a["L0_attn_rms_w"], (P, H))
    E = a["L0_ffn_b1"].shape[0]
    a["L0_ffn_b1"] = a["L0_ffn_b1"].reshape(E, -1, P).transpose(0, 2, 1)
    a["L0_ffn_b2"] = np.repeat(a["L0_ffn_b2"][:, None, :], P, axis=1)

    nc = bacc.Bacc("TRN2", target_bir_lowering=False, num_devices=1)
    arrays, args = {}, []
    for n in _IN:
        arrays[n] = np.ascontiguousarray(a[n])
        args.append(nc.dram_tensor(n, arrays[n].shape, mybir.dt.from_np(arrays[n].dtype), kind="ExternalInput").ap())
    shape = arrays["L0_attn_x"].shape
    args.append(nc.dram_tensor("out", shape, mybir.dt.float32, kind="ExternalOutput").ap())
    build(nc, *args)
    r = run_bass_kernel_spmd(nc, [arrays], core_ids=[0])
    return r.results[0]["out"]
```
